# Optimizing a Trainium2 kernel written in Bass

```python
import numpy as np
import jax
import jax.numpy as jnp

def _softmax(x, axis=-1):
    return jax.nn.softmax(x, axis=axis)

def _gelu(x):
    return jax.nn.gelu(x, approximate=True)

def _silu(x):
    return jax.nn.silu(x)

def _sigmoid(x):
    return jax.nn.sigmoid(x)

def _layernorm(x, axis=-1, eps=1e-05):
    m = jnp.mean(x, axis=axis, keepdims=True)
    v = jnp.var(x, axis=axis, keepdims=True)
    return (x - m) / jnp.sqrt(v + eps)

def _scatter_add(tgt, idx, src, axis=0):
    return tgt.at[idx].add(src)

def _segment_sum(src, seg, n):
    return jax.ops.segment_sum(src, seg, n)
kernel_name = 'mk_prb_d1_jaxref_r2_8673b1'

def setup_inputs(seed: int=0):
    np.random.seed(seed)
    _w = jnp.asarray

    def _L0_attn_setup():
        import jax, jax.numpy as jnp
        import numpy as np
        DIMS, HEAD = (512, 16)
        HD = DIMS // HEAD
        MAX_ITER = 3
        B, T = (4, 1024)

        def _ln(x, w, eps=1e-05):
            m = jnp.mean(x, axis=-1, keepdims=True)
            v = jnp.var(x, axis=-1, keepdims=True)
            return (x - m) * jax.lax.rsqrt(v + eps) * w
        key = jax.random.key(seed)
        ks = jax.random.split(key, 10)
        n = lambda k, s: jax.random.normal(k, s, jnp.float32) * 0.02
        z = lambda s: jnp.zeros(s, jnp.float32)
        o = lambda s: jnp.ones(s, jnp.float32)
        return {'x': jax.random.normal(ks[0], (B, T, DIMS), jnp.float32), 'Wq': n(ks[1], (DIMS, DIMS)), 'bq': z((DIMS,)), 'Wk': n(ks[2], (DIMS, DIMS)), 'Wv': n(ks[3], (DIMS, DIMS)), 'bv': z((DIMS,)), 'Wo': n(ks[4], (DIMS, DIMS)), 'bo': z((DIMS,)), 'lna_w': o((DIMS,)), 'lnc_w': o((HD,)), 'lnd_w': o((HD,)), 'Wlq': n(ks[5], (HD, HD)), 'blq': z((HD,)), 'Wlk': n(ks[6], (HD, HD)), 'blk': z((HD,)), 'Wlv': n(ks[7], (HD, HD)), 'blv': z((HD,)), 'temp': jnp.float32(1.0), 'threshold': jnp.float32(0.01), 'factor': jnp.float32(0.1)}
    _L0_attn_in = _L0_attn_setup()

    def _L0_ffn_setup():
        import jax, jax.numpy as jnp
        import numpy as np
        D_MODEL = 512
        M = 64
        INNER = 16
        key = jax.random.key(seed)
        ks = jax.random.split(key, 9)

        def init(k, shape, fan_in):
            bound = 1.0 / np.sqrt(fan_in)
            return jax.random.uniform(k, shape, jnp.float32, -bound, bound)
        x = jax.random.normal(ks[0], (16, 2048, D_MODEL), dtype=jnp.float32)
        Win = init(ks[1], (D_MODEL, M), D_MODEL)
        bin_ = init(ks[2], (M,), D_MODEL)
        W1 = init(ks[3], (M, INNER), 1)
        b1 = init(ks[4], (M, INNER), 1)
        W2 = init(ks[5], (M, INNER), INNER)
        b2 = init(ks[6], (M,), INNER)
        Wout = init(ks[7], (M, D_MODEL), M)
        bout = init(ks[8], (D_MODEL,), M)
        return {'x': x, 'Win': Win, 'bin_': bin_, 'W1': W1, 'b1': b1, 'W2': W2, 'b2': b2, 'Wout': Wout, 'bout': bout}
    _L0_ffn_in = _L0_ffn_setup()
    _d = {'L0_attn_x': _L0_attn_in['x'], 'L0_attn_Wq': _L0_attn_in['Wq'], 'L0_attn_bq': _L0_attn_in['bq'], 'L0_attn_Wk': _L0_attn_in['Wk'], 'L0_attn_Wv': _L0_attn_in['Wv'], 'L0_attn_bv': _L0_attn_in['bv'], 'L0_attn_Wo': _L0_attn_in['Wo'], 'L0_attn_bo': _L0_attn_in['bo'], 'L0_attn_lna_w': _L0_attn_in['lna_w'], 'L0_attn_lnc_w': _L0_attn_in['lnc_w'], 'L0_attn_lnd_w': _L0_attn_in['lnd_w'], 'L0_attn_Wlq': _L0_attn_in['Wlq'], 'L0_attn_blq': _L0_attn_in['blq'], 'L0_attn_Wlk': _L0_attn_in['Wlk'], 'L0_attn_blk': _L0_attn_in['blk'], 'L0_attn_Wlv': _L0_attn_in['Wlv'], 'L0_attn_blv': _L0_attn_in['blv'], 'L0_attn_temp': _L0_attn_in['temp'], 'L0_attn_threshold': _L0_attn_in['threshold'], 'L0_attn_factor': _L0_attn_in['factor'], 'L0_ffn_Win': _L0_ffn_in['Win'], 'L0_ffn_bin_': _L0_ffn_in['bin_'], 'L0_ffn_W1': _L0_ffn_in['W1'], 'L0_ffn_b1': _L0_ffn_in['b1'], 'L0_ffn_W2': _L0_ffn_in['W2'], 'L0_ffn_b2': _L0_ffn_in['b2'], 'L0_ffn_Wout': _L0_ffn_in['Wout'], 'L0_ffn_bout': _L0_ffn_in['bout']}
    _x0 = _d['L0_attn_x']
    _d['L0_attn_x'] = jax.random.normal(jax.random.fold_in(jax.random.key(seed), 1), (4, 4096, 512), dtype=_x0.dtype)
    del _x0
    return _d

def reference(L0_attn_x, L0_attn_Wq, L0_attn_bq, L0_attn_Wk, L0_attn_Wv, L0_attn_bv, L0_attn_Wo, L0_attn_bo, L0_attn_lna_w, L0_attn_lnc_w, L0_attn_lnd_w, L0_attn_Wlq, L0_attn_blq, L0_attn_Wlk, L0_attn_blk, L0_attn_Wlv, L0_attn_blv, L0_attn_temp, L0_attn_threshold, L0_attn_factor, L0_ffn_Win, L0_ffn_bin_, L0_ffn_W1, L0_ffn_b1, L0_ffn_W2, L0_ffn_b2, L0_ffn_Wout, L0_ffn_bout):

    def _L0_attn_ref(x, Wq, bq, Wk, Wv, bv, Wo, bo, lna_w, lnc_w, lnd_w, Wlq, blq, Wlk, blk, Wlv, blv, temp, threshold, factor):
        import jax, jax.numpy as jnp
        import numpy as np
        DIMS, HEAD = (512, 16)
        HD = DIMS // HEAD
        MAX_ITER = 3
        B, T = (4, 1024)

        def _ln(x, w, eps=1e-05):
            m = jnp.mean(x, axis=-1, keepdims=True)
            v = jnp.var(x, axis=-1, keepdims=True)
            return (x - m) * jax.lax.rsqrt(v + eps) * w
        Bn, Tn, D = x.shape
        H, hd = (HEAD, HD)
        temp0 = jax.lax.stop_gradient(temp)
        thr = jax.lax.stop_gradient(threshold)
        fac = jax.lax.stop_gradient(factor)
        scale = hd ** (-0.25)
        xn = _ln(x, lna_w)
        q = (xn @ Wq.T + bq) * scale
        k = xn @ Wk.T * scale
        v = xn @ Wv.T + bv
        shp = lambda t: t.reshape(Bn, Tn, H, hd).transpose(0, 2, 1, 3)
        q, k, v = (shp(q), shp(k), shp(v))
        E = H
        sm_scale = 1.0 / float(np.sqrt(hd))
        qcur, kcur, vcur = (q, k, v)
        prev = jnp.zeros_like(q)
        attn_out = jnp.zeros_like(q)
        done = jnp.asarray(False)
        for it in range(MAX_ITER):
            ql = qcur[:, :, :E] @ Wlq.T + blq
            kl = kcur[:, :, :E] @ Wlk.T + blk
            vl = vcur[:, :, :E] @ Wlv.T + blv
            t_it = temp0 + 0.005 * it
            tscale = jnp.where((t_it != 1.0) & (t_it > 0), jax.lax.rsqrt(t_it), 1.0)
            qs = _ln(ql, lnc_w) * tscale
            ks_ = _ln(kl, lnd_w)
            logits = jnp.einsum('bhqd,bhkd->bhqk', qs, ks_) * sm_scale
            ai = jnp.einsum('bhqk,bhkd->bhqd', jax.nn.softmax(logits, axis=-1), vl)
            iter_out = jnp.zeros_like(qcur).at[:, :, :E].set(ai)
            diff = jnp.mean(jnp.abs(iter_out - prev))
            attn_out = jnp.where(done, attn_out, iter_out)
            done = done | (diff < thr + fac * diff) & (it > 0)
            prev = iter_out
            qcur = qcur + iter_out
            kcur, vcur = (kl, vl)
        out = attn_out.transpose(0, 2, 1, 3).reshape(Bn, Tn, D)
        return out @ Wo.T + bo

    def _L0_ffn_ref(x, Win, bin_, W1, b1, W2, b2, Wout, bout):
        import jax, jax.numpy as jnp
        import numpy as np
        D_MODEL = 512
        M = 64
        INNER = 16
        s = jnp.einsum('btd,dm->btm', x, Win) + bin_
        h = jax.nn.relu(s[..., None] * W1 + b1)
        g = jnp.einsum('btmh,mh->btm', h, W2) + b2
        out = jnp.einsum('btm,md->btd', g, Wout) + bout
        return out
    x = L0_attn_x
    xn = _layernorm(x, axis=-1)
    x = x + _L0_attn_ref(xn, L0_attn_Wq, L0_attn_bq, L0_attn_Wk, L0_attn_Wv, L0_attn_bv, L0_attn_Wo, L0_attn_bo, L0_attn_lna_w, L0_attn_lnc_w, L0_attn_lnd_w, L0_attn_Wlq, L0_attn_blq, L0_attn_Wlk, L0_attn_blk, L0_attn_Wlv, L0_attn_blv, L0_attn_temp, L0_attn_threshold, L0_attn_factor) + _L0_ffn_ref(xn, L0_ffn_Win, L0_ffn_bin_, L0_ffn_W1, L0_ffn_b1, L0_ffn_W2, L0_ffn_b2, L0_ffn_Wout, L0_ffn_bout)
    return x

_drawn_inputs = setup_inputs


def setup_inputs(seed=0):
    import zlib

    import numpy as np

    out = dict(_drawn_inputs(seed))
    spreads = {'L0_attn_bq': (0.0, 0.8),
     'L0_attn_bv': (0.0, 0.8),
     'L0_attn_bo': (0.0, 0.1),
     'L0_attn_lna_w': (1.0, 0.6),
     'L0_attn_lnc_w': (1.0, 0.6),
     'L0_attn_lnd_w': (1.0, 0.6),
     'L0_attn_blq': (0.0, 0.8),
     'L0_attn_blk': (0.0, 0.8),
     'L0_attn_blv': (0.0, 0.8)}
    factors = {'L0_attn_Wq': 8.0,
     'L0_attn_Wk': 8.0,
     'L0_attn_Wv': 8.0,
     'L0_attn_Wo': 8.0,
     'L0_attn_Wlq': 8.0,
     'L0_attn_Wlk': 8.0,
     'L0_attn_Wlv': 8.0,
     'L0_ffn_bin_': 22.101}
    for name, (base, spread) in spreads.items():
        noise = np.random.default_rng([zlib.crc32(name.encode()), seed]).standard_normal(out[name].shape)
        drawn = base * np.exp(spread * noise) if base else spread * noise
        out[name] = jnp.asarray(drawn.astype(out[name].dtype))
    for name, factor in factors.items():
        out[name] = (out[name] * factor).astype(out[name].dtype)
    return out
```

```python
from contextlib import ExitStack

import concourse.bass as bass
from concourse import mybir

F32 = mybir.dt.float32
F32R = mybir.dt.float32r
ACT = mybir.ActivationFunctionType
ALU = mybir.AluOpType
AX = mybir.AxisListType

P = 128
RING = 3
SLOTS = 8
EPS = 1e-5
ROUNDS = 3


def residual_block(nc, x, Wq, bq, Wk, Wv, bv, Wo, bo, lna_w, lnc_w, lnd_w, Wlq, blq, Wlk, blk, Wlv, blv,
                   temp, threshold, factor, Win, bin_, W1, b1, W2, b2, Wout, bout, out):
    B, T, D = x.shape
    M, INNER = W1.shape
    HD = Wlq.shape[0]
    H = D // HD
    DC = D // P
    TPP = 8
    BLK = TPP // 2 * P
    PAIR = 2 * BLK
    N_PAIRS = B * T // PAIR
    HK = INNER // 2
    assert 2 * M == P and HK == SLOTS and D == 512 and N_PAIRS >= 7

    x_v = x.rearrange("b (n p j) d -> (b n) p (j d)", p=P, j=TPP)
    out_v = out.rearrange("b (n p j) d -> (b n) p (j d)", p=P, j=TPP)

    ctx = ExitStack()
    with ctx:
        def sb(name, shape, dt=F32):
            return ctx.enter_context(nc.sbuf_tensor(name, shape, dt))

        def sem(name):
            return ctx.enter_context(nc.semaphore(name))

        pe, act, dve, pool, sp = nc.tensor, nc.scalar, nc.vector, nc.gpsimd, nc.sync

        x_sb = [sb(f"x{r}", [P, TPP * D]) for r in range(RING)]
        o_sb = [sb(f"o{r}", [P, TPP * D]) for r in range(RING)]
        xT = sb("xT", [P, DC, PAIR])
        S = [sb(f"S{r}", [P, PAIR]) for r in range(RING)]
        Hr = [sb(f"H{i}", [P, PAIR]) for i in range(4)]
        G = [sb(f"G{r}", [P, PAIR], F32R) for r in range(RING)]
        R = sb("R", [P, BLK])
        stats = sb("stats", [P, TPP, 6])
        dmean = sb("dmean", [P, TPP])
        m2 = sb("m2", [P, TPP])
        dm2 = sb("dm2", [P, TPP])
        veps = sb("veps", [P, TPP])
        rstd = sb("rstd", [P, TPP])
        rwide = sb("rwide", [P, TPP // 2, 2, M])

        ident = sb("ident", [P, P])
        istack = sb("istack", [P, M])
        nhalf = sb("nhalf", [P, 16])
        win = sb("win", [P, DC, M])
        w1c = sb("w1c", [P, HK])
        b1c = sb("b1c", [P, HK])
        w2c = sb("w2c", [P, HK])
        binc = sb("binc", [P, 1])
        b2c = sb("b2c", [P, 1])
        w2s = sb("w2s", [P, HK, M])
        wout_hi = sb("wout_hi", [P, D], F32R)
        wout_lo = sb("wout_lo", [P, D], F32R)
        bias_row = sb("bias_row", [P, D])
        ones_d = sb("ones_d", [P, P])

        bank = [ctx.enter_context(nc.psum_tensor(f"bank{i}", [P, 512], F32)) for i in range(8)]
        T_ps, s_ps, g_ps, o_ps = bank[0:2], bank[2], bank[3:6], bank[6:8]

        ld = [[sem(f"ld{r}{h}") for h in range(2)] for r in range(RING)]
        st = [[sem(f"st{r}{h}") for h in range(2)] for r in range(RING)]
        tr_done, ev_done = sem("tr_done"), sem("ev_done")
        sc_done = sem("sc_done")
        bn_done, var_done, rstd_done = sem("bn_done"), sem("var_done"), sem("rstd_done")
        rb_done, R_done, S_done = sem("rb_done"), sem("R_done"), sem("S_done")
        relu_done, g_done = sem("relu_done"), sem("g_done")
        hi_done, lo_done = sem("hi_done"), sem("lo_done")
        op_done, xc_done, add_done = sem("op_done"), sem("xc_done"), sem("add_done")

        count = {}
        line = {id(e): sem(f"line_{n}") for e, n in ((pe, "pe"), (act, "act"), (dve, "dve"), (pool, "pool"))}

        def tick(eng, ins):
            count[id(eng)] = count.get(id(eng), 0) + 1
            ins.then_inc(line[id(eng)], 1)
            return line[id(eng)], count[id(eng)]

        def after(eng, *marks):
            for s, v in marks:
                eng.wait_ge(s, v)

        dma_sems = {}

        def arrive(name, eng, *copies):
            s = sem(f"in_{name}")
            with nc.allow_non_contiguous_dma(reason="small parameters"):
                for dst, src in copies:
                    eng.dma_start(dst, src).then_inc(s, 16)
            return s, 16 * len(copies)

        col = lambda v: v.rearrange("(p o) -> p o", o=1)

        HALF = TPP // 2 * D

        def rows(view, n, h):
            c = slice(h * HALF, (h + 1) * HALF)
            return view[n, :, c] if isinstance(n, int) else view[bass.ds(n, 1), :, c].rearrange("o p m -> p (o m)")

        def load(q, m, h):
            n = RING * q + m
            if not isinstance(q, int) or q > 0:
                sp.wait_ge(xc_done, SLOTS * (n - RING) + 4 * (h + 1))
            sp.dma_start(x_sb[m][:, h * HALF:(h + 1) * HALF], rows(x_v, n, h)).then_inc(ld[m][h], 16)

        LT = H
        RW = B * LT
        xa = S[0][0:RW, 0:D]
        in_xa = arrive("xa", sp, *[(xa[b * LT:(b + 1) * LT, :], x[b, 0:LT, :]) for b in range(B)])
        w_nat = {}
        in_w = {}
        for i, (name, w) in enumerate((("q", Wq), ("k", Wk), ("v", Wv), ("o", Wo))):
            w_nat[name] = o_sb[i // 2][:, (i % 2) * DC * D:(i % 2 + 1) * DC * D].rearrange("p (c i) -> p c i", c=DC)
            in_w[name] = arrive(f"w{name}", sp, (w_nat[name], w.rearrange("(c p) i -> p c i", p=P)))
        load(0, 0, 0)
        load(0, 0, 1)
        NV = 5
        small = sb("small", [HD, 3 * HD + NV])
        in_small = arrive(
            "small", act,
            *[(small[:, i * HD:(i + 1) * HD], w) for i, w in enumerate((Wlq, Wlk, Wlv))],
            *[(small[:, 3 * HD + i:3 * HD + i + 1], col(v)) for i, v in enumerate((blq, blk, blv, lnc_w, lnd_w))])
        lna = S[0][0:RW, D:2 * D]
        in_lna = arrive("lna", act, (lna[:, :], lna_w.partition_broadcast(RW)))
        bqc = sb("bqc", [P, DC])
        bvc = sb("bvc", [P, DC])
        in_bq = arrive("bq", act, (bqc[:, :], bq.rearrange("(c p) -> p c", p=P)), (bvc[:, :], bv.rearrange("(c p) -> p c", p=P)))
        scal = sb("scal", [P, 3])
        in_scal = arrive("scal", act, *[(scal[:, i:i + 1], v.partition_broadcast(P)) for i, v in enumerate((temp, threshold, factor))])
        in_win = arrive("win", act, (win[:, :, :], Win.rearrange("(c p) m -> p c m", p=P)))
        in_ffn = arrive("ffn", act, *[
            cp for f in range(2) for cp in (
                (w1c[f * M:(f + 1) * M, :], W1[:, f * HK:(f + 1) * HK]),
                (b1c[f * M:(f + 1) * M, :], b1[:, f * HK:(f + 1) * HK]),
                (w2c[f * M:(f + 1) * M, :], W2[:, f * HK:(f + 1) * HK]),
                (binc[f * M:(f + 1) * M, :], col(bin_)),
                (b2c[f * M:(f + 1) * M, :], col(b2)))])
        wo2 = S[2][:, 0:D]
        in_wo2 = arrive("wo2", act, (wo2[0:M, :], Wout), (wo2[M:P, :], Wout))
        row1 = S[1][:, D:2 * D]
        in_rows = arrive("rows", act, (bias_row[:, :], bout.partition_broadcast(P)), (row1[:, :], bo.partition_broadcast(P)))
        for m in (1, 2):
            load(0, m, 0)
            load(0, m, 1)

        block4 = sb("block4", [P, P])
        cmask = sb("cmask", [P, RW])
        half2 = sb("half2", [P, 2])
        epsc = sb("epsc", [P, 1])
        z = tick(pool, pool.memset(ident[:, :], 0.0))
        tick(pool, pool.memset(nhalf[:, :], -0.5))
        tick(pool, pool.memset(epsc[:, :], EPS))
        tick(pool, pool.memset(ones_d[:, :], 1.0))
        tick(pool, pool.memset(cmask[:, :], 0.0))
        tick(pool, pool.memset(half2[:, :], 1.0))
        z = tick(pool, pool.memset(block4[:, :], 1.0))
        after(pool, z)
        mk_ident = tick(pool, pool.affine_select(out=ident[:, :], in_=ident[:, :], compare_op=ALU.not_equal, fill=1.0,
                                                 base=0, pattern=[[-1, P]], channel_multiplier=1))
        hpc = P // HD

        def band(ap, width, groups, inner, fill):
            after(pool, tick(pool, pool.affine_select(out=ap, in_=ap, compare_op=ALU.is_ge, fill=fill, base=0,
                                                      pattern=[[-width, groups], [0, inner]], channel_multiplier=1)))
            t = tick(pool, pool.affine_select(out=ap, in_=ap, compare_op=ALU.is_ge, fill=fill, base=width - 1,
                                              pattern=[[width, groups], [0, inner]], channel_multiplier=-1))
            after(pool, t)
            return t

        band(block4[:, :].rearrange("p (g i) -> p g i", g=hpc), HD, hpc, HD, 0.0)
        band(half2[:, :].rearrange("p (g i) -> p g i", g=2), P // 2, 2, 1, 0.0)
        for f in range(2):
            mk_pool = band(cmask[f * RW:(f + 1) * RW, :].rearrange("p (g i) -> p g i", g=B), LT, B, LT, -1e30)
        assert 2 * RW == P

        after(pe, mk_pool, in_win)
        for c in range(DC):
            mm = pe.matmul(bank[7][:, 0:M], ones_d[:, :], win[:, c, :], start=(c == 0), stop=(c == DC - 1))
        t = tick(pe, mm)
        wmean = sb("wmean", [P, M])
        after(dve, t, in_win, in_ffn, in_wo2, in_rows, mk_pool)
        t = tick(dve, dve.tensor_scalar(wmean[:, :], bank[7][:, 0:M], 1.0 / D, None, ALU.mult))
        t2 = tick(dve, dve.tensor_tensor(istack[:, :], ident[:, 0:M], ident[:, M:P], ALU.add))
        t3 = tick(dve, dve.tensor_scalar(b1tmp := sb("b1tmp", [P, HK])[:, :], w1c[:, :], binc[:, 0:1], None, ALU.mult))
        t4 = tick(dve, dve.tensor_copy(wout_hi[:, :], wo2[:, :]))
        tick(dve, dve.tensor_tensor(bias_row[:, :], bias_row[:, :], row1[:, :], ALU.add))
        after(dve, t4)
        tick(dve, dve.tensor_tensor(win[:, :, :], win[:, :, :], wmean[:, :].unsqueeze(1).to_broadcast([P, DC, M]), ALU.subtract))
        for k in range(HK):
            tick(dve, dve.tensor_scalar(w2s[:, k, :], istack[:, :], w2c[:, k:k + 1], None, ALU.mult))
        tick(dve, dve.tensor_tensor(b1c[:, :], b1tmp, b1c[:, :], ALU.add))
        consts = tick(dve, dve.tensor_tensor(wout_lo[:, :], wo2[:, :], wout_hi[:, :].bitcast(F32), ALU.subtract))

        SM = float(HD) ** -0.5
        QS = float(HD) ** -0.25
        flat = lambda t: t.rearrange("p a b -> p (a b)")
        mv = sb("mv", [RW, 8])
        ms = sb("ms", [RW, 16])
        xn = S[1][0:RW, 0:D]

        def row_norm(src, dst, marks):
            after(dve, *marks)
            a = tick(dve, dve.bn_stats(mv[:, 0:6], src))
            after(dve, a)
            a = tick(dve, dve.bn_aggr(ms[:, 0:2], mv[:, 0:6]))
            after(dve, a)
            a = tick(dve, dve.tensor_scalar(ms[:, 2:3], ms[:, 1:2], EPS, None, ALU.add))
            after(pool, a)
            a = tick(pool, pool.tensor_tensor(ms[:, 3:4], ms[:, 2:3], nhalf[0:RW, 0:1], ALU.pow))
            after(dve, a)
            return tick(dve, dve.tensor_scalar(dst, src, ms[:, 0:1], ms[:, 3:4], ALU.subtract, ALU.mult))

        a = row_norm(xa[:, :], xn[:, :], (in_xa, mk_pool))
        a = row_norm(xn[:, :], xa[:, :], (a,))
        after(dve, a, in_lna)
        xn_done = tick(dve, dve.tensor_tensor(xn[:, :], xa[:, :], lna[:, :], ALU.mult))

        W_T = [xT[:, u // 2, (u % 2) * D:(u % 2 + 1) * D] if u < 2 * DC else
               Hr[(u - 2 * DC) // 2][:, (u % 2) * D:(u % 2 + 1) * D] for u in range(4 * DC)]
        evacs = []
        for i, name in enumerate("qkvo"):
            after(pe, in_w[name], mk_ident)
            for ic in range(DC):
                u = i * DC + ic
                if u >= 4:
                    after(pe, evacs[u - 4])
                for oc in range(DC):
                    mm = pe.transpose(bank[u % 4][:, oc * P:(oc + 1) * P], w_nat[name][:, oc, ic * P:(ic + 1) * P], ident[:, :])
                t = tick(pe, mm)
                if u % 2:
                    after(act, t)
                    evacs.append(tick(act, act.activation(W_T[u], bank[u % 4][:, :], ACT.Copy)))
                else:
                    after(dve, t)
                    evacs.append(tick(dve, dve.tensor_copy(W_T[u], bank[u % 4][:, :])))

        xnT = S[2][:, D:D + DC * RW].rearrange("p (c r) -> p c r", c=DC)
        after(pe, xn_done)
        for c in range(DC):
            mm = pe.transpose(bank[4][:, c * RW:(c + 1) * RW], xn[:, c * P:(c + 1) * P], ident[0:RW, 0:RW])
        a = tick(pe, mm)
        after(act, a)
        a = tick(act, act.activation(flat(xnT[:, :, :]), bank[4][:, 0:DC * RW], ACT.Copy))
        after(pe, a, *evacs[-4:])
        CR = DC * RW
        for i in range(3):
            ps = bank[5] if i < 2 else bank[6]
            for oc in range(DC):
                at = (i % 2) * CR + oc * RW
                for ic in range(DC):
                    mm = pe.matmul(ps[:, at:at + RW], W_T[i * DC + ic][:, oc * P:(oc + 1) * P], xnT[:, ic, :],
                                   start=(ic == 0), stop=(ic == DC - 1))
        a = tick(pe, mm)
        qT = sb("qT", [P, DC, RW])
        kT = sb("kT", [P, CR])
        vT = sb("vT", [P, DC, 2, RW])
        wide = lambda c: c.unsqueeze(2).to_broadcast([P, DC, RW])
        chunks = lambda t: t.rearrange("p (c r) -> p c r", c=DC)
        after(dve, a, in_bq)
        t = tick(dve, dve.tensor_scalar(bqs := sb("bqs", [P, DC])[:, :], bqc[:, :], QS, None, ALU.mult))
        tick(dve, dve.tensor_scalar(kT[:, :], bank[5][:, CR:2 * CR], QS, None, ALU.mult))
        tick(dve, dve.tensor_tensor(vT[:, :, 0, :], chunks(bank[6][:, 0:CR]), wide(bvc[:, :]), ALU.add))
        after(dve, t)
        qkv_done = tick(dve, dve.scalar_tensor_tensor(qT[:, :, :], chunks(bank[5][:, 0:CR]), QS, wide(bqs), ALU.mult, ALU.add))

        tile4 = sb("tile4", [HD, P])
        t = tick(dve, dve.tensor_copy(tile4[:, :].rearrange("p (h d) -> p h d", h=hpc),
                                      ident[0:HD, 0:HD].unsqueeze(1).to_broadcast([HD, hpc, HD])))
        after(pe, t)
        after(pe, in_small, mk_pool)
        t = tick(pe, pe.matmul(bank[7][:, 0:3 * HD + NV], tile4[:, :], small[:, :], start=True, stop=True))
        rep = sb("rep", [P, 3 * HD + NV])
        centre = sb("centre", [P, P])
        avg = sb("avg", [P, P])
        nat = sb("nat", [P, 3, P])
        after(dve, t)
        t = tick(dve, dve.tensor_copy(rep[:, :], bank[7][:, 0:3 * HD + NV]))
        u = tick(dve, dve.tensor_scalar(avg[:, :], block4[:, :], 1.0 / HD, None, ALU.mult))
        after(dve, u)
        tick(dve, dve.tensor_tensor(centre[:, :], ident[:, :], avg[:, :], ALU.subtract))
        heads = lambda t: t.rearrange("p (h d) -> p h d", h=hpc)
        for i in range(3):
            t = tick(dve, dve.tensor_tensor(heads(nat[:, i, :]), rep[:, i * HD:(i + 1) * HD].unsqueeze(1).to_broadcast([P, hpc, HD]),
                                            heads(block4[:, :]), ALU.mult))
        after(pe, t)
        bd = sb("bd", [P, 4, P])
        for j, (i, rhs) in enumerate(((0, centre), (1, centre), (1, ident), (2, ident))):
            pe.matmul(bank[7][:, j * P:(j + 1) * P], nat[:, i, :], rhs[:, :], start=True, stop=True)
        t = tick(pe, pe.matmul(bank[4][:, 0:2], centre[:, :], rep[:, 3 * HD:3 * HD + 2], start=True, stop=True))
        after(dve, t)
        tick(dve, dve.tensor_copy(flat(bd[:, :, :]), bank[7][:, :]))
        bqk = sb("bqk", [P, 2])
        tick(dve, dve.tensor_copy(bqk[:, :], bank[4][:, 0:2]))
        blkv = rep[:, 3 * HD + 1:3 * HD + 3]
        hmask = sb("hmask", [P, hpc])
        tick(dve, dve.tensor_scalar(hmask[:, :], block4[:, ::HD], rep[:, 3 * HD + 4:3 * HD + 5], None, ALU.mult))
        tt = sb("tt", [P, 4, ROUNDS])
        for it in range(ROUNDS):
            t = tick(dve, dve.tensor_scalar(tt[:, 0, it:it + 1], scal[:, 0:1], 0.005 * it, None, ALU.add)) if it else None
            if it == 0:
                after(dve, in_scal)
                t = tick(dve, dve.tensor_copy(tt[:, 0, 0:1], scal[:, 0:1]))
        after(dve, t)
        t = tick(dve, dve.tensor_scalar(tt[:, 1, :], tt[:, 0, :], 0.0, None, ALU.is_gt))
        after(dve, t)
        t = tick(dve, dve.tensor_scalar(tt[:, 2, :], tt[:, 0, :], 1.0, None, ALU.subtract))
        after(dve, t)
        t = tick(dve, dve.tensor_tensor(tt[:, 2, :], tt[:, 2, :], tt[:, 1, :], ALU.mult))
        after(dve, t)
        t = tick(dve, dve.tensor_scalar(tt[:, 2, :], tt[:, 2, :], 1.0, None, ALU.add))
        after(pool, t)
        t = tick(pool, pool.tensor_tensor(tt[:, 3, :], tt[:, 2, :], nhalf[:, 0:ROUNDS], ALU.pow))
        after(dve, t)
        wq_it = sb("wq_it", [P, ROUNDS])
        round_consts = tick(dve, dve.tensor_scalar(wq_it[:, :], tt[:, 3, :], rep[:, 3 * HD + 3:3 * HD + 4], None, ALU.mult))

        qk = sb("qk", [P, 2, CR])
        sq = sb("sq", [P, 2 * CR])
        kbd = sb("kbd", [P, DC, hpc, RW])
        lg = sb("lg", [P, H // 2, RW])
        ex = sb("ex", [P, H // 2, RW])
        AT = sb("AT", [P, 4, P])
        Vbd = sb("Vbd", [P, H // 2, 2, HD])
        red = sb("red", [P, 3, H // 2])
        ai = [sb(f"ai{i}", [P, CR]) for i in range(ROUNDS)]
        dsum = sb("dsum", [P, 8])
        q_mark = kv_mark = qkv_done
        for it in range(ROUNDS):
            after(pe, q_mark, kv_mark, round_consts)
            pe.matmul(bank[0][:, 0:CR], bd[:, 0, :], flat(qT[:, :, :]), start=True, stop=True)
            pe.matmul(bank[0][:, CR:2 * CR], bd[:, 1, :], kT[:, :], start=True, stop=True)
            a = tick(pe, pe.matmul(bank[1][:, CR:2 * CR], bd[:, 3, :], vT[:, :, 0, :], start=True, stop=True))
            b = a
            b = tick(pe, pe.matmul(bank[1][:, 0:CR], bd[:, 2, :], kT[:, :], start=True, stop=True))
            after(dve, b)
            a = tick(dve, dve.tensor_tensor(qk[:, :, :], bank[0][:, :].rearrange("p (a c) -> p a c", a=2),
                                            bqk[:, :].unsqueeze(2).to_broadcast([P, 2, CR]), ALU.add))
            tick(dve, dve.tensor_scalar(kT[:, :], bank[1][:, 0:CR], blkv[:, 0:1], None, ALU.add))
            kv_mark = tick(dve, dve.tensor_scalar(vT[:, :, :, :], chunks(bank[1][:, CR:2 * CR]).unsqueeze(2).to_broadcast([P, DC, 2, RW]),
                                                  blkv[:, 1:2], None, ALU.add))
            after(act, a)
            a = tick(act, act.activation(sq[:, :], flat(qk[:, :, :]), ACT.Square))
            after(pe, a)
            a = tick(pe, pe.matmul(bank[2][:, :], avg[:, :], sq[:, :], start=True, stop=True))
            after(act, a)
            a = tick(act, act.activation(sq[:, :], bank[2][:, :], ACT.Sqrt, bias=epsc[:, 0:1]))
            after(pe, kv_mark)
            for c in range(DC):
                mm = pe.transpose(bank[3][:, c * P:(c + 1) * P], vT[:, c, :, :].rearrange("p a r -> p (a r)"), ident[:, :])
            v_mark = tick(pe, mm)
            after(dve, a)
            a = tick(dve, dve.reciprocal(sq[:, :], sq[:, :]))
            after(dve, a)
            a = tick(dve, dve.tensor_tensor(flat(qk[:, :, :]), flat(qk[:, :, :]), sq[:, :], ALU.mult))
            after(dve, a)
            tick(dve, dve.tensor_tensor(kbd[:, :, :, :], chunks(qk[:, 1, :]).unsqueeze(2).to_broadcast([P, DC, hpc, RW]),
                                        hmask[:, :].unsqueeze(1).unsqueeze(3).to_broadcast([P, DC, hpc, RW]), ALU.mult))
            a = tick(dve, dve.tensor_scalar(qk[:, 0, :], qk[:, 0, :], wq_it[:, it:it + 1], None, ALU.mult))
            after(pe, a)
            for c in range(DC):
                f, w = c // 2, c % 2
                mm = pe.matmul(bank[4][f * RW:(f + 1) * RW, w * CR:(w + 1) * CR], qk[:, 0, c * RW:(c + 1) * RW],
                               kbd[:, c, :, :], start=True, stop=True)
            a = tick(pe, mm)
            after(dve, v_mark)
            tick(dve, dve.tensor_tensor(Vbd[:, :, :, :], bank[3][:, :].rearrange("p (g a d) -> p g a d", a=2, d=HD),
                                        half2[:, :].unsqueeze(1).unsqueeze(3).to_broadcast([P, H // 2, 2, HD]), ALU.mult))
            after(dve, a)
            heads8 = lambda t: t.rearrange("p (h r) -> p h r", r=RW)
            a = tick(dve, dve.tensor_tensor(lg[:, :, :], heads8(bank[4][:, :]), cmask[:, :].unsqueeze(1).to_broadcast([P, H // 2, RW]), ALU.add))
            after(dve, a)
            a = tick(dve, dve.tensor_reduce(red[:, 0, :], lg[:, :, :], AX.X, ALU.max))
            after(dve, a)
            a = tick(dve, dve.tensor_tensor(lg[:, :, :], lg[:, :, :], red[:, 0, :].unsqueeze(2).to_broadcast([P, H // 2, RW]), ALU.subtract))
            after(act, a)
            a = tick(act, act.activation(flat(ex[:, :, :]), flat(lg[:, :, :]), ACT.Exp, scale=SM))
            after(dve, a)
            a = tick(dve, dve.tensor_reduce(red[:, 1, :], ex[:, :, :], AX.X, ALU.add))
            after(dve, a)
            a = tick(dve, dve.reciprocal(red[:, 2, :], red[:, 1, :]))
            after(dve, a)
            a = tick(dve, dve.tensor_tensor(ex[:, :, :], ex[:, :, :], red[:, 2, :].unsqueeze(2).to_broadcast([P, H // 2, RW]), ALU.mult))
            after(pe, a)
            for j in range(4):
                mm = pe.transpose(bank[5][:, j * P:(j + 1) * P], ex[:, 2 * j:2 * j + 2, :].rearrange("p a b -> p (a b)"), ident[:, :])
            a = tick(pe, mm)
            after(act, a)
            a = tick(act, act.activation(flat(AT[:, :, :]), bank[5][:, :], ACT.Copy))
            after(pe, a)
            for g in range(H // 2):
                f, j = g // 4, g % 4
                mm = pe.matmul(bank[6][(g % 2) * RW:(g % 2 + 1) * RW, (g // 2) * RW:(g // 2 + 1) * RW],
                               Vbd[:, g, :, :].rearrange("p a d -> p (a d)"), AT[:, j, f * RW:(f + 1) * RW], start=True, stop=True)
            a = tick(pe, mm)
            after(dve, a)
            ai_mark = tick(dve, dve.tensor_copy(ai[it][:, :], bank[6][:, 0:CR]))
            q_mark = tick(dve, dve.tensor_tensor(flat(qT[:, :, :]), flat(qT[:, :, :]), bank[6][:, 0:CR], ALU.add))

        after(dve, ai_mark)
        a = tick(dve, dve.tensor_tensor(sq[:, 0:CR], ai[1][:, :], ai[0][:, :], ALU.subtract))
        after(act, a)
        a = tick(act, act.activation(sq[:, CR:2 * CR], sq[:, 0:CR], ACT.Abs, accum_out=dsum[:, 0:1]))
        after(pe, a)
        a = tick(pe, pe.matmul(bank[7][:, 0:1], ones_d[:, :], dsum[:, 0:1], start=True, stop=True))
        after(dve, a)
        a = tick(dve, dve.tensor_scalar(dsum[:, 1:2], bank[7][:, 0:1], 1.0 / (B * H * T * HD), None, ALU.mult))
        after(dve, a)
        a = tick(dve, dve.tensor_scalar(dsum[:, 2:3], dsum[:, 1:2], scal[:, 2:3], scal[:, 1:2], ALU.mult, ALU.add))
        after(dve, a)
        a = tick(dve, dve.tensor_tensor(dsum[:, 3:4], dsum[:, 1:2], dsum[:, 2:3], ALU.is_lt))
        after(dve, a)
        a = tick(dve, dve.tensor_scalar(dsum[:, 4:5], dsum[:, 3:4], -1.0, 1.0, ALU.mult, ALU.add))
        after(dve, a)
        a = tick(dve, dve.tensor_scalar(ai[2][:, :], ai[2][:, :], dsum[:, 4:5], None, ALU.mult))
        after(dve, a)
        a = tick(dve, dve.scalar_tensor_tensor(ai[1][:, :], ai[1][:, :], dsum[:, 3:4], ai[2][:, :], ALU.mult, ALU.add))
        after(pe, a)
        for c in range(DC):
            mm = pe.matmul(bank[7][0:RW, :], ai[1][:, c * RW:(c + 1) * RW], W_T[3 * DC + c], start=(c == 0), stop=(c == DC - 1))
        a = tick(pe, mm)
        att = sb("att", [RW, D])
        after(act, a)
        att_done = tick(act, act.activation(att[:, :], bank[7][0:RW, :], ACT.Copy))

        def at(q, m):
            return RING * q + m

        def outside(q, m):
            return isinstance(q, int) and not 0 <= at(q, m) < N_PAIRS

        def positive(v):
            return not isinstance(v, int) or v > 0

        def wait(eng, s, v):
            if positive(v):
                eng.wait_ge(s, v)

        def transpose(q, m, k):
            c, b = k // 2, k % 2
            n = at(q, m)
            if k < 2:
                wait(pe, ld[m][k], 16 * (q + 1))
            wait(pe, ev_done, SLOTS * n + k - 1)
            for j in range(4):
                col0 = (4 * b + j) * D + c * P
                mm = pe.transpose(T_ps[k % 2][:, j * P:(j + 1) * P], x_sb[m][:, col0:col0 + P], ident[:, :])
            mm.then_inc(tr_done, 1)

        def evacuate(q, m, k):
            c, b = k // 2, k % 2
            n = at(q, m)
            wait(act, tr_done, SLOTS * n + k + 1)
            wait(act, sc_done, 4 * (n - 1) + c + 1)
            act.activation(xT[:, c, b * BLK:(b + 1) * BLK], T_ps[k % 2][:, :], ACT.Copy).then_inc(ev_done, 1)

        def s_product(q, m, c):
            n = at(q, m)
            wait(pe, ev_done, SLOTS * n + 2 * c + 2)
            if c == 0:
                wait(pe, S_done, 4 * n)
            for b in range(2):
                mm = pe.matmul(s_ps[b * M:(b + 1) * M, :], win[:, c, :], xT[:, c, b * BLK:(b + 1) * BLK],
                               start=(c == 0), stop=(c == DC - 1))
            mm.then_inc(sc_done, 1)

        def statistics(q, m, j):
            n = at(q, m)
            if j % 4 == 0:
                wait(dve, ld[m][j // 4], 16 * (q + 1))
            dve.bn_stats(stats[:, j, :], x_sb[m][:, j * D:(j + 1) * D]).then_inc(bn_done, 1)

        def variance(q, m):
            n = at(q, m)
            base = (TPP + 3) * n + TPP
            wait(dve, bn_done, base)
            dve.tensor_tensor(dmean[:, :], stats[:, :, 1], stats[:, :, 4], ALU.subtract).then_inc(bn_done, 1)
            dve.scalar_tensor_tensor(m2[:, :], stats[:, :, 2], D * EPS, stats[:, :, 5], ALU.add, ALU.add).then_inc(bn_done, 1)
            wait(dve, bn_done, base + 1)
            dve.scalar_tensor_tensor(dm2[:, :], dmean[:, :], 0.25, dmean[:, :], ALU.mult, ALU.mult).then_inc(bn_done, 1)
            wait(dve, bn_done, base + 3)
            dve.scalar_tensor_tensor(veps[:, :], m2[:, :], 1.0 / D, dm2[:, :], ALU.mult, ALU.add).then_inc(var_done, 1)

        def inv_std(q, m):
            n = at(q, m)
            wait(pool, var_done, n + 1)
            pool.tensor_tensor(rstd[:, :], veps[:, :], nhalf[:, 0:TPP], ALU.pow).then_inc(rstd_done, 1)
            wait(pool, rstd_done, 2 * n + 1)
            pool.tensor_tensor(rwide[:, :, :, :], rstd[:, :].rearrange("p (b j) -> p j b", b=2).unsqueeze(3)
                               .to_broadcast([P, TPP // 2, 2, M]),
                               ones_d[:, :].rearrange("p (b m) -> p b m", b=2).unsqueeze(1).to_broadcast([P, TPP // 2, 2, M]),
                               ALU.mult).then_inc(rstd_done, 1)

        def spread_rstd(q, m):
            n = at(q, m)
            wait(pe, rstd_done, 2 * n + 2)
            for j in range(4):
                mm = pe.transpose(g_ps[m][:, j * P:(j + 1) * P], rwide[:, j, :, :].rearrange("p b m -> p (b m)"), ident[:, :])
            mm.then_inc(rb_done, 1)

        def copy_rstd(q, m):
            n = at(q, m)
            wait(act, rb_done, n + 1)
            wait(act, S_done, 4 * n)
            act.activation(R[:, :], g_ps[m][:, :], ACT.Copy).then_inc(R_done, 1)

        def scale_s(q, m):
            n = at(q, m)
            wait(dve, sc_done, 4 * n + 4)
            wait(dve, R_done, n + 1)
            for b in range(2):
                for f in range(2):
                    dve.tensor_tensor(S[m][f * M:(f + 1) * M, b * BLK:(b + 1) * BLK], s_ps[b * M:(b + 1) * M, :],
                                      R[b * M:(b + 1) * M, :], ALU.mult).then_inc(S_done, 1)

        def relu(q, m, k):
            n = at(q, m)
            if k == 0:
                wait(act, S_done, 4 * n + 4)
            wait(act, g_done, SLOTS * n + k - 3)
            act.activation(Hr[k % 4][:, :], S[m][:, :], ACT.Relu, bias=b1c[:, k:k + 1], scale=w1c[:, k:k + 1]).then_inc(relu_done, 1)

        def sum_h(q, m, k):
            n = at(q, m)
            wait(pe, relu_done, SLOTS * n + k + 1)
            for b in range(2):
                mm = pe.matmul(g_ps[m][b * M:(b + 1) * M, :], w2s[:, k, :], Hr[k % 4][:, b * BLK:(b + 1) * BLK],
                               start=(k == 0), stop=(k == HK - 1))
            mm.then_inc(g_done, 1)

        def g_high(q, m):
            n = at(q, m)
            wait(act, g_done, SLOTS * n + SLOTS)
            for b in range(2):
                r = slice(b * M, (b + 1) * M)
                act.activation(G[m][r, b * BLK:(b + 1) * BLK], g_ps[m][r, :], ACT.Identity, bias=b2c[r, 0:1]).then_inc(hi_done, 1)

        def g_low(q, m):
            n = at(q, m)
            for b in range(2):
                wait(dve, hi_done, 2 * n + b + 1)
                r, o, cs = slice(b * M, (b + 1) * M), slice((1 - b) * M, (2 - b) * M), slice(b * BLK, (b + 1) * BLK)
                dve.scalar_tensor_tensor(G[m][o, cs], g_ps[m][r, :], b2c[r, 0:1], G[m][r, cs].bitcast(F32),
                                         ALU.add, ALU.subtract).then_inc(lo_done, 1)

        def project(q, m, j):
            n = at(q, m)
            if j == 0:
                wait(pe, lo_done, 2 * n + 2)
            wait(pe, add_done, SLOTS * n + j - 1)
            pe.matmul(o_ps[j % 2][:, :], G[m][:, j * P:(j + 1) * P], wout_hi[:, :], start=True, stop=False)
            pe.matmul(o_ps[j % 2][:, :], G[m][:, j * P:(j + 1) * P], wout_lo[:, :], start=False, stop=True).then_inc(op_done, 1)

        def add_bias(q, m, j):
            n = at(q, m)
            if j % 4 == 0:
                wait(pool, ld[m][j // 4], 16 * (q + 1))
                wait(pool, st[m][j // 4], 16 * q)
                wait(pool, tr_done, SLOTS * n + SLOTS)
            c = slice(j * D, (j + 1) * D)
            pool.tensor_tensor(o_sb[m][:, c], x_sb[m][:, c], bias_row[:, :], ALU.add).then_inc(xc_done, 1)

        def add(q, m, j):
            n = at(q, m)
            wait(dve, op_done, SLOTS * n + j + 1)
            wait(dve, xc_done, SLOTS * n + j + 1)
            c = slice(j * D, (j + 1) * D)
            dve.tensor_tensor(o_sb[m][:, c], o_sb[m][:, c], o_ps[j % 2][:, :], ALU.add).then_inc(add_done, 1)

        def store(q, m, h):
            n = at(q, m)
            wait(sp, add_done, SLOTS * n + 4 * (h + 1))
            sp.dma_start(rows(out_v, n, h), o_sb[m][:, h * HALF:(h + 1) * HALF]).then_inc(st[m][h], 16)

        S_PRODUCT = (3, 5, 7, 8)
        STATISTICS = ((0, 1), (2, 3), (), (4,), (), (5, 6), (7,), ())
        VARIANCE, INV_STD, SPREAD, COPY_R, SCALE = 7, 7, 8, 9, 10
        RELU, SUM_H, SPLIT, PROJECT, ADD, BIAS = 11, 12, 20, 21, 22, 8

        def run(stage, q, m, k, first, width=1):
            for back in range(4):
                j = k + SLOTS * back - first
                if 0 <= j < width:
                    mm = m - back
                    qq = q + mm // RING
                    if not outside(qq, mm % RING):
                        stage(qq, mm % RING, *((j,) if width > 1 else ()))

        def body(q, m):
            for k in range(SLOTS):
                run(transpose, q, m, k, 0, SLOTS)
                run(spread_rstd, q, m, k, SPREAD)
                run(sum_h, q, m, k, SUM_H, SLOTS)
                for c, slot in enumerate(S_PRODUCT):
                    run(lambda a, b: s_product(a, b, c), q, m, k, slot)
                run(project, q, m, k, PROJECT, SLOTS)
                run(evacuate, q, m, k, 0, SLOTS)
                run(copy_rstd, q, m, k, COPY_R)
                run(g_high, q, m, k, SPLIT)
                run(relu, q, m, k, RELU, SLOTS)
                run(scale_s, q, m, k, SCALE)
                run(g_low, q, m, k, SPLIT)
                for j in STATISTICS[k]:
                    run(lambda a, b: statistics(a, b, j), q, m, k, k)
                run(variance, q, m, k, VARIANCE)
                run(add, q, m, k, ADD, SLOTS)
                run(inv_std, q, m, k, INV_STD)
                run(add_bias, q, m, k, BIAS, SLOTS)

        after(pe, consts, att_done)
        after(act, consts)
        after(dve, consts)
        after(pool, consts)
        BODIES = N_PAIRS + 3
        LEAD = RING + 1
        LOOP = (N_PAIRS - LEAD) // RING
        for b in range(LEAD):
            body(b // RING, b % RING)
        with nc.Fori(1, 1 + LOOP, engines=[e.engine for e in (pe, act, dve, pool)]) as i:
            for b in range(1, 1 + RING):
                body(i + b // RING, b % RING)
        for b in range(LEAD + RING * LOOP, BODIES):
            body(b // RING, b % RING)

        def traffic(q, m):
            qs, ms = q - 1, m
            ql, ml = q + (m + 2) // RING, (m + 2) % RING
            for h in range(2):
                if not outside(qs, ms):
                    store(qs, ms, h)
                if not outside(ql, ml) and (not isinstance(ql, int) or ql > 0):
                    load(ql, ml, h)

        LOOP_SP = (N_PAIRS - 2 - RING) // RING
        for m in range(RING):
            traffic(0, m)
        with sp.Fori(1, 1 + LOOP_SP) as i:
            for m in range(RING):
                traffic(i, m)
        for b in range(RING * (1 + LOOP_SP), BODIES):
            traffic(b // RING, b % RING)

        after(pool, att_done)
        for m in range(RING):
            for h in range(2):
                pool.wait_ge(st[m][h], 16 * len(range(m, N_PAIRS, RING)))
        acc = sem("acc")
        for b in range(B):
            pool.dma_start(out[b, 0:LT, :], att[b * LT:(b + 1) * LT, :], accum_op=ALU.add).then_inc(acc, 16)
        pool.wait_ge(acc, 16 * B)


_INS = ['L0_attn_x', 'L0_attn_Wq', 'L0_attn_bq', 'L0_attn_Wk', 'L0_attn_Wv', 'L0_attn_bv', 'L0_attn_Wo', 'L0_attn_bo',
        'L0_attn_lna_w', 'L0_attn_lnc_w', 'L0_attn_lnd_w', 'L0_attn_Wlq', 'L0_attn_blq', 'L0_attn_Wlk', 'L0_attn_blk',
        'L0_attn_Wlv', 'L0_attn_blv', 'L0_attn_temp', 'L0_attn_threshold', 'L0_attn_factor',
        'L0_ffn_Win', 'L0_ffn_bin_', 'L0_ffn_W1', 'L0_ffn_b1', 'L0_ffn_W2', 'L0_ffn_b2', 'L0_ffn_Wout', 'L0_ffn_bout']


def kernel(**inputs):
    import numpy as _np
    import concourse.bacc as _bacc
    from concourse import mybir as _mybir
    from concourse.bass_utils import run_bass_kernel_spmd as _run

    nc = _bacc.Bacc("TRN2", target_bir_lowering=False, num_devices=1)
    arrays, args = {}, []
    for name in _INS:
        a = _np.ascontiguousarray(_np.atleast_1d(inputs[name]))
        arrays[f"in_{name}_dram"] = a
        args.append(nc.dram_tensor(f"in_{name}_dram", a.shape, _mybir.dt.from_np(a.dtype), kind="ExternalInput").ap())
    shape = inputs['L0_attn_x'].shape
    args.append(nc.dram_tensor("out_0_dram", shape, _mybir.dt.float32, kind="ExternalOutput").ap())
    residual_block(nc, *args)
    r = _run(nc, [arrays], core_ids=[0])
    return r.results[0]["out_0_dram"]
```

```python
from contextlib import ExitStack

import concourse.bass as bass
from concourse import mybir

F32 = mybir.dt.float32
F32R = mybir.dt.float32r
ACT = mybir.ActivationFunctionType
ALU = mybir.AluOpType
AX = mybir.AxisListType

P = 128
RING = 3
SLOTS = 8
STEPS = ((2,) * 8, (1,) * 8)
EPS = 1e-5
ROUNDS = 3


def residual_block(nc, x, Wq, bq, Wk, Wv, bv, Wo, bo, lna_w, lnc_w, lnd_w, Wlq, blq, Wlk, blk, Wlv, blv,
                   temp, threshold, factor, Win, bin_, W1, b1, W2, b2, Wout, bout, out):
    B, T, D = x.shape
    M, INNER = W1.shape
    HD = Wlq.shape[0]
    H = D // HD
    DC = D // P
    TPP = 8
    BLK = TPP // 2 * P
    PAIR = 2 * BLK
    N_PAIRS = B * T // PAIR
    MH = M // 2
    HG = P // MH
    HK = INNER // HG
    assert 2 * M == P and 2 * HK == SLOTS and D == 512 and N_PAIRS >= 7

    x_v = x.rearrange("b (n p j) d -> (b n) p (j d)", p=P, j=TPP)
    out_v = out.rearrange("b (n p j) d -> (b n) p (j d)", p=P, j=TPP)

    ctx = ExitStack()
    with ctx:
        def sb(name, shape, dt=F32):
            return ctx.enter_context(nc.sbuf_tensor(name, shape, dt))

        def sem(name):
            return ctx.enter_context(nc.semaphore(name))

        pe, act, dve, pool, sp = nc.tensor, nc.scalar, nc.vector, nc.gpsimd, nc.sync

        x_sb = [sb(f"x{r}", [P, TPP * D]) for r in range(RING)]
        o_sb = [sb(f"o{r}", [P, TPP * D]) for r in range(RING)]
        xT = sb("xT", [P, DC, PAIR])
        s_full = sb("s_full", [P, BLK])
        SH = sb("SH", [P, PAIR], F32R)
        Hr = [[sb(f"H{a}{i}", [P, PAIR]) for i in range(n)] for a, n in enumerate((HK, 3))]
        G = [sb(f"G{r}", [P, PAIR], F32R) for r in range(RING)]
        stats = sb("stats", [P, TPP, 6])
        dmean = sb("dmean", [P, TPP])
        m2 = sb("m2", [P, TPP])
        dm2 = sb("dm2", [P, TPP])
        veps = sb("veps", [P, TPP])
        rstd = sb("rstd", [P, TPP])
        rwide = sb("rwide", [P, TPP // 2, 2, M])

        ident = sb("ident", [P, P])
        istack = sb("istack", [P, MH])
        spread = sb("spread", [P, 2, P], F32R)
        nhalf = sb("nhalf", [P, 16])
        win = sb("win", [P, DC, M])
        w1c = sb("w1c", [P, 2, HK])
        b1c = sb("b1c", [P, 2, HK])
        w2c = sb("w2c", [P, 2, HK])
        binc = sb("binc", [P, 2])
        b2c = sb("b2c", [P, 1])
        w2s = sb("w2s", [P, 2, HK, MH])
        wout_hi = sb("wout_hi", [P, D], F32R)
        wout_lo = sb("wout_lo", [P, D], F32R)
        bias_row = sb("bias_row", [P, D])
        ones_d = sb("ones_d", [P, P])

        def ps(name, banks=1):
            return ctx.enter_context(nc.psum_tensor(name, [P, banks * 512], F32))

        T_ps, s_ps, g_ps, o_ps, rep_ps = [ps("T0"), ps("T1")], ps("s"), ps("g"), [ps("op0"), ps("op1")], ps("rep", 2)

        ld = [[sem(f"ld{r}{h}") for h in range(2)] for r in range(RING)]
        st = [[sem(f"st{r}{h}") for h in range(2)] for r in range(RING)]
        tr_done, ev_done = sem("tr_done"), sem("ev_done")
        sc_done = sem("sc_done")
        bn_done, var_done, rstd_done = sem("bn_done"), sem("var_done"), sem("rstd_done")
        rb_done, R_done, s_done = sem("rb_done"), sem("R_done"), sem("s_done")
        sh_done, sl_done = sem("sh_done"), sem("sl_done")
        rep_done = sem("rep_done")
        relu_done, g_done = sem("relu_done"), sem("g_done")
        hi_done, lo_done = sem("hi_done"), sem("lo_done")
        op_done, xc_done, add_done = sem("op_done"), sem("xc_done"), sem("add_done")

        count = {}
        line = {id(e): sem(f"line_{n}") for e, n in ((pe, "pe"), (act, "act"), (dve, "dve"), (pool, "pool"))}

        def tick(eng, ins):
            count[id(eng)] = count.get(id(eng), 0) + 1
            ins.then_inc(line[id(eng)], 1)
            return line[id(eng)], count[id(eng)]

        def after(eng, *marks):
            for s, v in marks:
                eng.wait_ge(s, v)

        dma_sems = {}

        def arrive(name, eng, *copies):
            s = sem(f"in_{name}")
            with nc.allow_non_contiguous_dma(reason="small parameters"):
                for dst, src in copies:
                    eng.dma_start(dst, src).then_inc(s, 16)
            return s, 16 * len(copies)

        col = lambda v: v.rearrange("(p o) -> p o", o=1)

        HALF = TPP // 2 * D

        def rows(view, n, h):
            c = slice(h * HALF, (h + 1) * HALF)
            return view[n, :, c] if isinstance(n, int) else view[bass.ds(n, 1), :, c].rearrange("o p m -> p (o m)")

        def load(q, m, h):
            n = RING * q + m
            if not isinstance(q, int) or q > 0:
                sp.wait_ge(xc_done, SLOTS * (n - RING) + 4 * (h + 1))
            sp.dma_start(x_sb[m][:, h * HALF:(h + 1) * HALF], rows(x_v, n, h)).then_inc(ld[m][h], 16)

        LT = H
        RW = B * LT
        CR = DC * RW
        hpc = P // HD
        H2 = H // 2
        assert 2 * RW == P
        flat = lambda t: t.rearrange("p a b -> p (a b)")

        xa, lna = Hr[0][1][0:RW, 0:D], Hr[0][1][0:RW, D:2 * D]
        wo2, row1 = Hr[0][0][:, 0:D], Hr[0][0][:, D:2 * D]
        w_nat = {n: o_sb[i // 2][:, (i % 2) * DC * D:(i % 2 + 1) * DC * D].rearrange("p (c i) -> p c i", c=DC)
                 for i, n in enumerate("qkvo")}
        W_T = {"q": o_sb[2][:, 0:DC * D], "k": o_sb[2][:, DC * D:2 * DC * D],
               "v": sb("WvT", [P, DC * D])[:, :], "o": sb("WoT", [P, DC * D])[:, :]}
        W_T = {n: w.rearrange("p (c o) -> p c o", c=DC) for n, w in W_T.items()}
        NV = 5
        small = sb("small", [HD, 3 * HD + NV])
        bqc = sb("bqc", [P, DC])
        bvc = sb("bvc", [P, DC])
        scal = sb("scal", [P, 3])

        load(0, 0, 0)
        in_win = arrive("win", sp, (win[:, :, :], Win.rearrange("(c p) m -> p c m", p=P)))
        load(0, 0, 1)
        in_xa = arrive("xa", sp, *[(xa[b * LT:(b + 1) * LT, :], x[b, 0:LT, :]) for b in range(B)])
        in_small = arrive(
            "small", act,
            *[(small[:, i * HD:(i + 1) * HD], w) for i, w in enumerate((Wlq, Wlk, Wlv))],
            *[(small[:, 3 * HD + i:3 * HD + i + 1], col(v)) for i, v in enumerate((blq, blk, blv, lnc_w, lnd_w))])
        in_lna = arrive("lna", sp, (lna, lna_w.partition_broadcast(RW)))
        in_w = {}

        def load_weight(n, w):
            in_w[n] = arrive(f"w{n}", sp, (w_nat[n], w.rearrange("(c p) i -> p c i", p=P)))

        load_weight("q", Wq)
        load(0, 1, 0)
        load_weight("k", Wk)
        load(0, 1, 1)
        by_g = lambda w, a: w[a * MH:(a + 1) * MH, :].rearrange("m (g h) -> g m h", g=HG)
        in_ffn = arrive(
            "ffn", sp,
            *[(dst[:, a, :], by_g(src, a)) for dst, src in ((w1c, W1), (b1c, b1), (w2c, W2)) for a in range(2)],
            *[(binc[g * MH:(g + 1) * MH, :], bin_.rearrange("(a m) -> m a", a=2)) for g in range(HG)],
            *[(b2c[f * M:(f + 1) * M, :], col(b2)) for f in range(2)])
        in_wo2 = arrive("wo2", sp, (wo2[0:M, :], Wout), (wo2[M:P, :], Wout))
        in_rows = arrive("rows", sp, (bias_row[:, :], bout.partition_broadcast(P)), (row1, bo.partition_broadcast(P)))
        load_weight("v", Wv)
        load_weight("o", Wo)
        load(0, 2, 0)
        load(0, 2, 1)

        block4 = sb("block4", [P, P])
        cmask = sb("cmask", [P, RW])
        half2 = sb("half2", [P, 2])
        epsc = sb("epsc", [P, 1])
        z = tick(pool, pool.memset(ident[:, :], 0.0))
        after(pool, z)
        mk_ident = tick(pool, pool.affine_select(out=ident[:, :], in_=ident[:, :], compare_op=ALU.not_equal, fill=1.0,
                                                 base=0, pattern=[[-1, P]], channel_multiplier=1))
        mk_ones = tick(pool, pool.memset(ones_d[:, :], 1.0))
        tick(pool, pool.memset(nhalf[:, :], -0.5))
        tick(pool, pool.memset(epsc[:, :], EPS))
        tick(pool, pool.memset(cmask[:, :], 0.0))
        tick(pool, pool.memset(half2[:, :], 1.0))
        z = tick(pool, pool.memset(block4[:, :], 1.0))
        after(pool, z)

        def band(ap, width, groups, inner, fill):
            after(pool, tick(pool, pool.affine_select(out=ap, in_=ap, compare_op=ALU.is_ge, fill=fill, base=0,
                                                      pattern=[[-width, groups], [0, inner]], channel_multiplier=1)))
            t = tick(pool, pool.affine_select(out=ap, in_=ap, compare_op=ALU.is_ge, fill=fill, base=width - 1,
                                              pattern=[[width, groups], [0, inner]], channel_multiplier=-1))
            after(pool, t)
            return t

        band(block4[:, :].rearrange("p (g i) -> p g i", g=hpc), HD, hpc, HD, 0.0)
        band(half2[:, :].rearrange("p (g i) -> p g i", g=2), P // 2, 2, 1, 0.0)
        for f in range(2):
            mk_pool = band(cmask[f * RW:(f + 1) * RW, :].rearrange("p (g i) -> p g i", g=B), LT, B, LT, -1e30)

        wmean = sb("wmean", [P, M])
        after(pe, mk_ones, in_win)
        for c in range(DC):
            mm = pe.matmul(g_ps[:, 0:M], ones_d[:, :], win[:, c, :], start=(c == 0), stop=(c == DC - 1))
        t = tick(pe, mm)
        after(dve, t)
        t = tick(dve, dve.tensor_scalar(wmean[:, :], g_ps[:, 0:M], 1.0 / D, None, ALU.mult))
        after(dve, t)
        t = tick(dve, dve.tensor_tensor(win[:, :, :], win[:, :, :], wmean[:, :].unsqueeze(1).to_broadcast([P, DC, M]), ALU.subtract))
        after(pe, t, mk_ident)

        tmp = {n: sb(n, shape) for n, shape in (("isum", [P, M]), ("wb", [P, 2, HK]))}

        def constants():
            after(dve, mk_ident)
            a = tick(dve, dve.tensor_tensor(tmp["isum"][:, :], ident[:, 0:M], ident[:, M:P], ALU.add))
            after(dve, a)
            a = tick(dve, dve.tensor_tensor(istack[:, :], tmp["isum"][:, 0:MH], tmp["isum"][:, MH:M], ALU.add))
            for half in range(2):
                a = tick(dve, dve.tensor_copy(spread[:, half, :].rearrange("p (g m) -> p g m", g=HG),
                                              tmp["isum"][:, half * MH:(half + 1) * MH].unsqueeze(1).to_broadcast([P, HG, MH])))
            yield
            after(dve, a, in_ffn)
            a = tick(dve, dve.tensor_tensor(tmp["wb"][:, :, :], w1c[:, :, :], binc[:, :].unsqueeze(2).to_broadcast([P, 2, HK]), ALU.mult))
            after(dve, a)
            tick(dve, dve.tensor_tensor(b1c[:, :, :], tmp["wb"][:, :, :], b1c[:, :, :], ALU.add))
            for half in range(2):
                for k in range(HK):
                    a = tick(dve, dve.tensor_scalar(w2s[:, half, k, :], istack[:, :], w2c[:, half, k:k + 1], None, ALU.mult))
            after(pe, a)
            after(act, a)
            yield
            after(dve, in_wo2, in_rows)
            a = tick(dve, dve.tensor_copy(wout_hi[:, :], wo2))
            b = tick(dve, dve.tensor_tensor(bias_row[:, :], bias_row[:, :], row1, ALU.add))
            after(dve, a)
            a = tick(dve, dve.tensor_tensor(wout_lo[:, :], wo2, wout_hi[:, :].bitcast(F32), ALU.subtract))
            after(pool, b)
            after(pe, a)
            after(act, a)
            result["constants"] = True
            yield

        SM = float(HD) ** -0.5
        QS = float(HD) ** -0.25
        mv = sb("mv", [RW, 8])
        ms = sb("ms", [RW, 16])
        xn_all = sb("xn", [P, D])
        xn = xn_all[0:RW, :]
        xnT = sb("xnT", [P, DC, RW])
        qkn = sb("qkn", [P, D])
        sq = sb("vn", [P, D])
        vn = sq[0:RW, :]
        qT = sb("qT", [P, DC, RW])
        kT = sb("kT", [P, CR])
        vT = sb("vT", [P, DC, 2, RW])
        bqs = sb("bqs", [P, DC])
        tile4 = sb("tile4", [HD, P])
        rep = sb("repw", [P, 3 * HD + NV])
        centre = sb("centre", [P, P])
        avg = sb("avg", [P, P])
        nat = sb("nat", [P, 3, P])
        bd = sb("bd", [P, 4, P])
        bqk = sb("bqk", [P, 2])
        hmask = sb("hmask", [P, hpc])
        tt = sb("tt", [P, 4, ROUNDS])
        wq_it = sb("wq_it", [P, ROUNDS])
        qk = sb("qk", [P, 2, CR])
        over_v = flat(W_T["v"])
        kbd = over_v[:, 0:hpc * CR].rearrange("p (c h r) -> p c h r", c=DC, h=hpc)
        lg = over_v[:, hpc * CR:(hpc + 2) * CR].rearrange("p (h r) -> p h r", r=RW)
        AT = over_v[:, (hpc + 2) * CR:(hpc + 4) * CR].rearrange("p (a b) -> p a b", a=4)
        Vbd = qkn[:, :].rearrange("p (g a d) -> p g a d", a=2, d=HD)
        red = sb("red", [P, 3, H2])
        ai = [xn_all[:, 0:CR], xn_all[:, CR:2 * CR], flat(xnT[:, :, :])]
        dsum = sb("dsum", [P, 8])
        att = vn
        chunks = lambda t: t.rearrange("p (c r) -> p c r", c=DC)
        wide = lambda c: c.unsqueeze(2).to_broadcast([P, DC, RW])
        heads = lambda t: t.rearrange("p (h d) -> p h d", h=hpc)
        heads8 = lambda t: t.rearrange("p (h r) -> p h r", r=RW)
        over8 = lambda t: t.unsqueeze(2).to_broadcast([P, H2, RW])
        A_ps = o_ps[1]
        result = {}

        def row_norm(src, dst, marks):
            after(dve, *marks)
            a = tick(dve, dve.bn_stats(mv[:, 0:6], src))
            after(dve, a)
            a = tick(dve, dve.bn_aggr(ms[:, 0:2], mv[:, 0:6]))
            after(dve, a)
            a = tick(dve, dve.tensor_scalar(ms[:, 2:3], ms[:, 1:2], EPS, None, ALU.add))
            after(pool, a)
            a = tick(pool, pool.tensor_tensor(ms[:, 3:4], ms[:, 2:3], nhalf[0:RW, 0:1], ALU.pow))
            yield
            after(dve, a)
            yield tick(dve, dve.tensor_scalar(dst, src, ms[:, 0:1], ms[:, 3:4], ALU.subtract, ALU.mult))

        def attention():
            a = None
            for src, dst in ((xa, xn[:, :]), (xn[:, :], xa)):
                for mark in row_norm(src, dst, (a or in_xa,)):
                    a = mark or a
                    yield
            after(dve, a, in_lna)
            xn_done = tick(dve, dve.tensor_tensor(xn[:, :], xa, lna, ALU.mult))
            after(act, xn_done)
            in_bq = arrive("bq", pool, (bqc[:, :], bq.rearrange("(c p) -> p c", p=P)), (bvc[:, :], bv.rearrange("(c p) -> p c", p=P)))
            in_scal = arrive("scal", pool, *[(scal[:, i:i + 1], v.partition_broadcast(P)) for i, v in enumerate((temp, threshold, factor))])

            banks = [rep_ps[:, 0:D], rep_ps[:, D:2 * D], o_ps[0][:, :], o_ps[1][:, :]]
            evacs = []

            def turn(n):
                after(pe, in_w[n])
                for ic in range(DC):
                    u = len(evacs)
                    if u >= 4:
                        after(pe, evacs[u - 4])
                    for oc in range(DC):
                        mm = pe.transpose(banks[u % 4][:, oc * P:(oc + 1) * P], w_nat[n][:, oc, ic * P:(ic + 1) * P], ident[:, :])
                    t = tick(pe, mm)
                    if u % 2:
                        after(act, t)
                        evacs.append(tick(act, act.activation(W_T[n][:, ic, :], banks[u % 4], ACT.Copy)))
                    else:
                        after(dve, t)
                        evacs.append(tick(dve, dve.tensor_copy(W_T[n][:, ic, :], banks[u % 4])))
                    if ic % 2:
                        yield

            after(pe, xn_done)
            for c in range(DC):
                mm = pe.transpose(g_ps[:, c * RW:(c + 1) * RW], xn[:, c * P:(c + 1) * P], ident[0:RW, 0:RW])
            a = tick(pe, mm)
            after(act, a)
            xnT_done = tick(act, act.activation(flat(xnT[:, :, :]), g_ps[:, 0:CR], ACT.Copy))
            yield
            yield from turn("q")
            yield from turn("k")
            after(pool, *evacs[-4:])
            result["k turned"] = True
            yield from constants()
            yield from turn("v")
            yield from turn("o")
            after(pool, *evacs[-4:])
            after(pe, *evacs[-4:])
            result["weights turned"] = True
            yield
            after(pe, xnT_done)
            for ic in range(DC):
                for i, n in enumerate("qk"):
                    mm = pe.matmul(g_ps[i * RW:(i + 1) * RW, :], xnT[:, ic, :], W_T[n][:, ic, :], start=(ic == 0), stop=(ic == DC - 1))
            a = tick(pe, mm)
            after(act, a)
            a = tick(act, act.activation(qkn[:, :], g_ps[:, :], ACT.Copy, scale=QS))
            yield
            after(pe, a)
            for ic in range(DC):
                mm = pe.matmul(g_ps[0:RW, :], xnT[:, ic, :], W_T["v"][:, ic, :], start=(ic == 0), stop=(ic == DC - 1))
            b = tick(pe, mm)
            after(act, b)
            b = tick(act, act.activation(vn[:, :], g_ps[0:RW, :], ACT.Copy))
            after(pool, b)
            after(pe, b)
            result["q, k, v"] = True
            yield
            for c in range(DC):
                mm = pe.transpose(A_ps[:, c * P:(c + 1) * P], qkn[:, c * P:(c + 1) * P], ident[:, :])
            a = tick(pe, mm)
            after(dve, in_bq)
            t = tick(dve, dve.tensor_scalar(bqs[:, :], bqc[:, :], QS, None, ALU.mult))
            after(dve, t, a)
            qk_ps = A_ps[:, :].rearrange("p (c a r) -> p c a r", c=DC, a=2)
            tick(dve, dve.tensor_tensor(qT[:, :, :], qk_ps[:, :, 0, :], wide(bqs[:, :]), ALU.add))
            a = tick(dve, dve.tensor_copy(chunks(kT[:, :]), qk_ps[:, :, 1, :]))
            yield
            after(pe, a)
            for c in range(DC):
                mm = pe.transpose(A_ps[:, c * RW:(c + 1) * RW], vn[:, c * P:(c + 1) * P], ident[0:RW, 0:RW])
            a = tick(pe, mm)
            after(dve, a)
            qkv_done = tick(dve, dve.tensor_tensor(vT[:, :, 0, :], chunks(A_ps[:, 0:CR]), wide(bvc[:, :]), ALU.add))
            yield

            after(dve, mk_pool)
            t = tick(dve, dve.tensor_copy(tile4[:, :].rearrange("p (h d) -> p h d", h=hpc),
                                          ident[0:HD, 0:HD].unsqueeze(1).to_broadcast([HD, hpc, HD])))
            a = tick(dve, dve.tensor_scalar(avg[:, :], block4[:, :], 1.0 / HD, None, ALU.mult))
            after(dve, a)
            tick(dve, dve.tensor_tensor(centre[:, :], ident[:, :], avg[:, :], ALU.subtract))
            after(pe, t, qkv_done, in_small)
            t = tick(pe, pe.matmul(A_ps[:, 0:3 * HD + NV], tile4[:, :], small[:, :], start=True, stop=True))
            yield
            after(dve, t)
            t = tick(dve, dve.tensor_copy(rep[:, :], A_ps[:, 0:3 * HD + NV]))
            after(dve, t)
            for i in range(3):
                t = tick(dve, dve.tensor_tensor(heads(nat[:, i, :]), rep[:, i * HD:(i + 1) * HD].unsqueeze(1).to_broadcast([P, hpc, HD]),
                                                heads(block4[:, :]), ALU.mult))
            yield
            after(pe, t)
            for j, (i, rhs) in enumerate(((0, centre), (1, centre), (1, ident), (2, ident))):
                mm = pe.matmul(A_ps[:, j * P:(j + 1) * P], nat[:, i, :], rhs[:, :], start=True, stop=True)
            t = tick(pe, mm)
            after(dve, t)
            t = tick(dve, dve.tensor_copy(flat(bd[:, :, :]), A_ps[:, :]))
            yield
            after(pe, t)
            t = tick(pe, pe.matmul(A_ps[:, 0:2], centre[:, :], rep[:, 3 * HD:3 * HD + 2], start=True, stop=True))
            after(dve, t, in_scal)
            a = tick(dve, dve.tensor_copy(bqk[:, :], A_ps[:, 0:2]))
            blkv = rep[:, 3 * HD + 1:3 * HD + 3]
            tick(dve, dve.tensor_scalar(hmask[:, :], block4[:, ::HD], rep[:, 3 * HD + 4:3 * HD + 5], None, ALU.mult))
            for it in range(ROUNDS):
                t = tick(dve, dve.tensor_scalar(tt[:, 0, it:it + 1], scal[:, 0:1], 0.005 * it, None, ALU.add))
            after(dve, t)
            tick(dve, dve.tensor_scalar(tt[:, 1, :], tt[:, 0, :], 0.0, None, ALU.is_gt))
            t = tick(dve, dve.tensor_scalar(tt[:, 2, :], tt[:, 0, :], 1.0, None, ALU.subtract))
            after(dve, t)
            t = tick(dve, dve.tensor_tensor(tt[:, 2, :], tt[:, 2, :], tt[:, 1, :], ALU.mult))
            after(dve, t)
            t = tick(dve, dve.tensor_scalar(tt[:, 2, :], tt[:, 2, :], 1.0, None, ALU.add))
            after(pool, t)
            t = tick(pool, pool.tensor_tensor(tt[:, 3, :], tt[:, 2, :], nhalf[:, 0:ROUNDS], ALU.pow))
            yield
            after(dve, t)
            t = tick(dve, dve.tensor_scalar(wq_it[:, :], tt[:, 3, :], rep[:, 3 * HD + 3:3 * HD + 4], None, ALU.mult))
            free = (t, a)
            for it in range(ROUNDS):
                after(pe, *free)
                pe.matmul(A_ps[:, 0:CR], bd[:, 0, :], flat(qT[:, :, :]), start=True, stop=True)
                a = tick(pe, pe.matmul(A_ps[:, CR:2 * CR], bd[:, 1, :], kT[:, :], start=True, stop=True))
                after(dve, a)
                qk_done = tick(dve, dve.tensor_tensor(qk[:, :, :], A_ps[:, :].rearrange("p (a c) -> p a c", a=2),
                                                      bqk[:, :].unsqueeze(2).to_broadcast([P, 2, CR]), ALU.add))
                yield
                after(pe, qk_done)
                pe.matmul(A_ps[:, 0:CR], bd[:, 2, :], kT[:, :], start=True, stop=True)
                a = tick(pe, pe.matmul(A_ps[:, CR:2 * CR], bd[:, 3, :], vT[:, :, 0, :], start=True, stop=True))
                after(act, qk_done)
                sq_done = tick(act, act.activation(sq[:, :], flat(qk[:, :, :]), ACT.Square))
                after(dve, a)
                tick(dve, dve.tensor_scalar(kT[:, :], A_ps[:, 0:CR], blkv[:, 0:1], None, ALU.add))
                a = tick(dve, dve.tensor_scalar(vT[:, :, :, :], chunks(A_ps[:, CR:2 * CR]).unsqueeze(2).to_broadcast([P, DC, 2, RW]),
                                                blkv[:, 1:2], None, ALU.add))
                yield
                after(pe, a, sq_done)
                a = tick(pe, pe.matmul(A_ps[:, :], avg[:, :], sq[:, :], start=True, stop=True))
                after(act, a)
                a = tick(act, act.activation(sq[:, :], A_ps[:, :], ACT.Sqrt, bias=epsc[:, 0:1]))
                yield
                after(pe, a)
                for c in range(DC):
                    mm = pe.transpose(A_ps[:, c * P:(c + 1) * P], vT[:, c, :, :].rearrange("p a r -> p (a r)"), ident[:, :])
                v_mark = tick(pe, mm)
                after(dve, a)
                a = tick(dve, dve.reciprocal(sq[:, :], sq[:, :]))
                yield
                after(dve, v_mark)
                v_mark = tick(dve, dve.tensor_tensor(Vbd[:, :, :, :], A_ps[:, :].rearrange("p (g a d) -> p g a d", a=2, d=HD),
                                                     half2[:, :].unsqueeze(1).unsqueeze(3).to_broadcast([P, H2, 2, HD]), ALU.mult))
                after(dve, a)
                a = tick(dve, dve.tensor_tensor(flat(qk[:, :, :]), flat(qk[:, :, :]), sq[:, :], ALU.mult))
                after(dve, a)
                tick(dve, dve.tensor_tensor(kbd[:, :, :, :], chunks(qk[:, 1, :]).unsqueeze(2).to_broadcast([P, DC, hpc, RW]),
                                            hmask[:, :].unsqueeze(1).unsqueeze(3).to_broadcast([P, DC, hpc, RW]), ALU.mult))
                a = tick(dve, dve.tensor_scalar(qk[:, 0, :], qk[:, 0, :], wq_it[:, it:it + 1], None, ALU.mult))
                yield
                after(pe, a)
                for w in range(2):
                    for f in range(2):
                        c = 2 * f + w
                        mm = pe.matmul(A_ps[f * RW:(f + 1) * RW, w * CR:(w + 1) * CR], qk[:, 0, c * RW:(c + 1) * RW],
                                       kbd[:, c, :, :], start=True, stop=True)
                a = tick(pe, mm)
                after(dve, a)
                a = tick(dve, dve.tensor_tensor(lg[:, :, :], heads8(A_ps[:, :]), cmask[:, :].unsqueeze(1).to_broadcast([P, H2, RW]), ALU.add))
                yield
                after(dve, a)
                a = tick(dve, dve.tensor_reduce(red[:, 0, :], lg[:, :, :], AX.X, ALU.max))
                after(dve, a)
                a = tick(dve, dve.tensor_tensor(lg[:, :, :], lg[:, :, :], over8(red[:, 0, :]), ALU.subtract))
                after(act, a)
                a = tick(act, act.activation(flat(lg[:, :, :]), flat(lg[:, :, :]), ACT.Exp, scale=SM))
                yield
                after(dve, a)
                a = tick(dve, dve.tensor_reduce(red[:, 1, :], lg[:, :, :], AX.X, ALU.add))
                after(dve, a)
                a = tick(dve, dve.reciprocal(red[:, 2, :], red[:, 1, :]))
                after(dve, a)
                a = tick(dve, dve.tensor_tensor(lg[:, :, :], lg[:, :, :], over8(red[:, 2, :]), ALU.mult))
                yield
                after(pe, a)
                for j in range(4):
                    mm = pe.transpose(A_ps[:, j * P:(j + 1) * P], lg[:, 2 * j:2 * j + 2, :].rearrange("p a b -> p (a b)"), ident[:, :])
                a = tick(pe, mm)
                after(act, a)
                a = tick(act, act.activation(flat(AT[:, :, :]), A_ps[:, :], ACT.Copy))
                yield
                after(pe, a, v_mark)
                for g in range(H2):
                    f, j = g // 4, g % 4
                    mm = pe.matmul(A_ps[(g % 2) * RW:(g % 2 + 1) * RW, (g // 2) * RW:(g // 2 + 1) * RW],
                                   Vbd[:, g, :, :].rearrange("p a d -> p (a d)"), AT[:, j, f * RW:(f + 1) * RW], start=True, stop=True)
                a = tick(pe, mm)
                after(dve, a)
                t = tick(dve, dve.tensor_copy(ai[it][:, :], A_ps[:, 0:CR]))
                free = (tick(dve, dve.tensor_tensor(flat(qT[:, :, :]), flat(qT[:, :, :]), A_ps[:, 0:CR], ALU.add)),)
                yield

            after(dve, t)
            a = tick(dve, dve.tensor_tensor(sq[:, 0:CR], ai[1][:, :], ai[0][:, :], ALU.subtract))
            after(act, a)
            a = tick(act, act.activation(sq[:, CR:2 * CR], sq[:, 0:CR], ACT.Abs, accum_out=dsum[:, 0:1]))
            after(pe, a, *free)
            a = tick(pe, pe.matmul(A_ps[:, 0:1], ones_d[:, :], dsum[:, 0:1], start=True, stop=True))
            yield
            after(dve, a)
            a = tick(dve, dve.tensor_scalar(dsum[:, 1:2], A_ps[:, 0:1], 1.0 / (B * H * T * HD), None, ALU.mult))
            after(dve, a)
            a = tick(dve, dve.tensor_scalar(dsum[:, 2:3], dsum[:, 1:2], scal[:, 2:3], scal[:, 1:2], ALU.mult, ALU.add))
            after(dve, a)
            a = tick(dve, dve.tensor_tensor(dsum[:, 3:4], dsum[:, 1:2], dsum[:, 2:3], ALU.is_lt))
            after(dve, a)
            a = tick(dve, dve.tensor_scalar(dsum[:, 4:5], dsum[:, 3:4], -1.0, 1.0, ALU.mult, ALU.add))
            after(dve, a)
            a = tick(dve, dve.tensor_scalar(ai[2][:, :], ai[2][:, :], dsum[:, 4:5], None, ALU.mult))
            after(dve, a)
            a = tick(dve, dve.scalar_tensor_tensor(ai[1][:, :], ai[1][:, :], dsum[:, 3:4], ai[2][:, :], ALU.mult, ALU.add))
            yield
            after(pe, a)
            for c in range(DC):
                mm = pe.matmul(A_ps[0:RW, :], ai[1][:, c * RW:(c + 1) * RW], W_T["o"][:, c, :], start=(c == 0), stop=(c == DC - 1))
            a = tick(pe, mm)
            after(act, a)
            result["att"] = tick(act, act.activation(att[:, :], A_ps[0:RW, :], ACT.Copy))
            after(pe, result["att"])
            yield

        def at(q, m):
            return RING * q + m

        def outside(q, m):
            return isinstance(q, int) and not 0 <= at(q, m) < N_PAIRS

        def positive(v):
            return not isinstance(v, int) or v > 0

        def wait(eng, s, v):
            if positive(v):
                eng.wait_ge(s, v)

        def need(name):
            while name not in result:
                next(side)

        def transpose(q, m, k):
            c, b = k // 2, k % 2
            n = at(q, m)
            if k < 2:
                wait(pe, ld[m][k], 16 * (q + 1))
            wait(pe, ev_done, SLOTS * n + k - 1)
            for j in range(4):
                col0 = (4 * b + j) * D + c * P
                mm = pe.transpose(T_ps[k % 2][:, j * P:(j + 1) * P], x_sb[m][:, col0:col0 + P], ident[:, :])
            mm.then_inc(tr_done, 1)

        def evacuate(q, m, k):
            c, b = k // 2, k % 2
            n = at(q, m)
            wait(act, tr_done, SLOTS * n + k + 1)
            wait(act, sc_done, 4 * (n - 1) + c + 1)
            act.activation(xT[:, c, b * BLK:(b + 1) * BLK], T_ps[k % 2][:, :], ACT.Copy).then_inc(ev_done, 1)

        def s_product(q, m, c):
            n = at(q, m)
            wait(pe, ev_done, SLOTS * n + 2 * c + 2)
            if c == 0:
                wait(pe, s_done, n)
            for b in range(2):
                mm = pe.matmul(s_ps[b * M:(b + 1) * M, :], win[:, c, :], xT[:, c, b * BLK:(b + 1) * BLK],
                               start=(c == 0), stop=(c == DC - 1))
            mm.then_inc(sc_done, 1)

        def statistics(q, m, j):
            n = at(q, m)
            if j % 4 == 0:
                wait(dve, ld[m][j // 4], 16 * (q + 1))
            dve.bn_stats(stats[:, j, :], x_sb[m][:, j * D:(j + 1) * D]).then_inc(bn_done, 1)

        def variance(q, m):
            n = at(q, m)
            base = (TPP + 3) * n + TPP
            wait(dve, bn_done, base)
            dve.tensor_tensor(dmean[:, :], stats[:, :, 1], stats[:, :, 4], ALU.subtract).then_inc(bn_done, 1)
            dve.scalar_tensor_tensor(m2[:, :], stats[:, :, 2], D * EPS, stats[:, :, 5], ALU.add, ALU.add).then_inc(bn_done, 1)
            wait(dve, bn_done, base + 1)
            dve.scalar_tensor_tensor(dm2[:, :], dmean[:, :], 0.25, dmean[:, :], ALU.mult, ALU.mult).then_inc(bn_done, 1)
            wait(dve, bn_done, base + 3)
            dve.scalar_tensor_tensor(veps[:, :], m2[:, :], 1.0 / D, dm2[:, :], ALU.mult, ALU.add).then_inc(var_done, 1)

        def inv_std(q, m):
            n = at(q, m)
            wait(pool, var_done, n + 1)
            pool.tensor_tensor(rstd[:, :], veps[:, :], nhalf[:, 0:TPP], ALU.pow).then_inc(rstd_done, 1)
            wait(pool, rstd_done, 2 * n + 1)
            pool.tensor_tensor(rwide[:, :, :, :], rstd[:, :].rearrange("p (b j) -> p j b", b=2).unsqueeze(3)
                               .to_broadcast([P, TPP // 2, 2, M]),
                               ones_d[:, :].rearrange("p (b m) -> p b m", b=2).unsqueeze(1).to_broadcast([P, TPP // 2, 2, M]),
                               ALU.mult).then_inc(rstd_done, 1)

        def spread_rstd(q, m):
            n = at(q, m)
            wait(pe, rstd_done, 2 * n + 2)
            need("q, k, v")
            wait(pe, lo_done, 2 * (n - 1))
            for j in range(4):
                mm = pe.transpose(g_ps[:, j * P:(j + 1) * P], rwide[:, j, :, :].rearrange("p b m -> p (b m)"), ident[:, :])
            mm.then_inc(rb_done, 1)

        def copy_rstd(q, m):
            n = at(q, m)
            wait(act, rb_done, n + 1)
            wait(act, sl_done, 2 * n)
            act.activation(s_full[:, :], g_ps[:, :], ACT.Copy).then_inc(R_done, 1)

        def scale_s(q, m):
            n = at(q, m)
            wait(dve, sc_done, 4 * n + 4)
            wait(dve, R_done, n + 1)
            dve.tensor_tensor(s_full[:, :], s_ps[:, :], s_full[:, :], ALU.mult).then_inc(s_done, 1)

        def halves(b):
            return slice(b * M, (b + 1) * M), slice((1 - b) * M, (2 - b) * M), slice(b * BLK, (b + 1) * BLK)

        def s_high(q, m):
            n = at(q, m)
            wait(act, s_done, n + 1)
            wait(act, rep_done, 2 * n)
            for b in range(2):
                own, _, cols = halves(b)
                act.activation(SH[own, cols], s_full[own, :], ACT.Copy).then_inc(sh_done, 1)

        def s_low(q, m):
            n = at(q, m)
            for b in range(2):
                own, other, cols = halves(b)
                wait(dve, sh_done, 2 * n + b + 1)
                dve.tensor_tensor(SH[other, cols], s_full[own, :], SH[own, cols].bitcast(F32), ALU.subtract).then_inc(sl_done, 1)

        def replicate(q, m, half):
            n = at(q, m)
            need("weights turned")
            if half == 0:
                wait(pe, sl_done, 2 * n + 2)
            wait(pe, relu_done, SLOTS * n + HK * half)
            for b in range(2):
                cols = slice(b * BLK, (b + 1) * BLK)
                mm = pe.matmul(rep_ps[:, cols], spread[:, half, :], SH[:, cols], start=True, stop=True)
            mm.then_inc(rep_done, 1)

        def relu(q, m, r):
            n, half, k = at(q, m), r // HK, r % HK
            need("constants")
            if k == 0:
                wait(act, rep_done, 2 * n + half + 1)
            if half == 0:
                wait(act, g_done, HK * (n - 1) + k + 1)
            else:
                wait(act, g_done, HK * (n - 1) + (HK, k + 1, k + 1, HK + 1)[k])
            act.activation(Hr[half][k % len(Hr[half])][:, :], rep_ps[:, :], ACT.Relu,
                           bias=b1c[:, half, k:k + 1], scale=w1c[:, half, k:k + 1]).then_inc(relu_done, 1)

        def sum_h(q, m, k):
            n = at(q, m)
            wait(pe, relu_done, SLOTS * n + HK + k + 1)
            if k == 0:
                if isinstance(n, int) and n == N_PAIRS - 1:
                    wait(pe, lo_done, 2 * n)
                else:
                    wait(pe, R_done, n + 2)
            for half in range(2):
                for b in range(2):
                    at0 = b * M + half * MH
                    mm = pe.matmul(g_ps[at0:at0 + MH, :], w2s[:, half, k, :],
                                   Hr[half][k % len(Hr[half])][:, b * BLK:(b + 1) * BLK], start=(k == 0), stop=(k == HK - 1),
                                   tile_position=(0, at0))
            mm.then_inc(g_done, 1)

        def g_high(q, m):
            n = at(q, m)
            wait(act, g_done, HK * n + HK)
            for b in range(2):
                own, _, cols = halves(b)
                act.activation(G[m][own, cols], g_ps[own, :], ACT.Identity, bias=b2c[own, 0:1]).then_inc(hi_done, 1)

        def g_low(q, m):
            n = at(q, m)
            for b in range(2):
                own, other, cols = halves(b)
                wait(dve, hi_done, 2 * n + b + 1)
                dve.scalar_tensor_tensor(G[m][other, cols], g_ps[own, :], b2c[own, 0:1], G[m][own, cols].bitcast(F32),
                                         ALU.add, ALU.subtract).then_inc(lo_done, 1)

        def product_bank(j):
            return o_ps[0 if attending else j % 2][:, :]

        def project(q, m, j):
            n = at(q, m)
            if j == 0:
                wait(pe, lo_done, 2 * n + 2)
            wait(pe, add_done, SLOTS * n + j - (0 if attending else 1))
            bank = product_bank(j)
            for part in (wout_hi, wout_lo):
                mm = pe.matmul(bank, G[m][:, j * P:(j + 1) * P], part[:, :], start=(part is wout_hi), stop=(part is wout_lo))
            mm.then_inc(op_done, 1)

        def add_bias(q, m, j):
            n = at(q, m)
            need(("k turned", "weights turned", "q, k, v")[m])
            need("constants")
            if j % 4 == 0:
                wait(pool, ld[m][j // 4], 16 * (q + 1))
                wait(pool, st[m][j // 4], 16 * q)
                wait(pool, tr_done, SLOTS * n + SLOTS)
            c = slice(j * D, (j + 1) * D)
            pool.tensor_tensor(o_sb[m][:, c], x_sb[m][:, c], bias_row[:, :], ALU.add).then_inc(xc_done, 1)

        def add(q, m, j):
            n = at(q, m)
            wait(dve, op_done, SLOTS * n + j + 1)
            wait(dve, xc_done, SLOTS * n + j + 1)
            c = slice(j * D, (j + 1) * D)
            dve.tensor_tensor(o_sb[m][:, c], o_sb[m][:, c], product_bank(j), ALU.add).then_inc(add_done, 1)

        def store(q, m, h):
            n = at(q, m)
            wait(sp, add_done, SLOTS * n + 4 * (h + 1))
            sp.dma_start(rows(out_v, n, h), o_sb[m][:, h * HALF:(h + 1) * HALF]).then_inc(st[m][h], 16)

        S_PRODUCT = (2, 7, 8, 9)
        STATISTICS = ((), (0, 1), (2,), (3, 4), (5,), (6, 7), (), ())
        VARIANCE, INV_STD, SPREAD, COPY_R, SCALE, HIGH, LOW = 5, 6, 8, 9, 10, 11, 12
        REPLICATE, RELU, SUM_H, G_HIGH, G_LOW, PROJECT, ADD, BIAS = (13, 17), 13, 19, 23, 24, 25, 26, 10

        def run(stage, q, m, k, first, width=1):
            for back in range(5):
                j = k + SLOTS * back - first
                if 0 <= j < width:
                    mm = m - back
                    qq = q + mm // RING
                    if not outside(qq, mm % RING):
                        stage(qq, mm % RING, *((j,) if width > 1 else ()))

        def body(q, m, steps=(0,) * SLOTS):
            for k in range(SLOTS):
                run(transpose, q, m, k, 0, SLOTS)
                for half in range(2):
                    run(lambda a, b: replicate(a, b, half), q, m, k, REPLICATE[half])
                run(project, q, m, k, PROJECT, SLOTS)
                run(sum_h, q, m, k, SUM_H, HK)
                for c, slot in enumerate(S_PRODUCT):
                    run(lambda a, b: s_product(a, b, c), q, m, k, slot)
                run(spread_rstd, q, m, k, SPREAD)
                run(s_high, q, m, k, HIGH)
                run(evacuate, q, m, k, 0, SLOTS)
                run(copy_rstd, q, m, k, COPY_R)
                run(relu, q, m, k, RELU, 2 * HK)
                run(g_high, q, m, k, G_HIGH)
                run(scale_s, q, m, k, SCALE)
                run(s_low, q, m, k, LOW)
                run(g_low, q, m, k, G_LOW)
                run(add, q, m, k, ADD, SLOTS)
                for j in STATISTICS[k]:
                    run(lambda a, b: statistics(a, b, j), q, m, k, k)
                run(variance, q, m, k, VARIANCE)
                run(inv_std, q, m, k, INV_STD)
                run(add_bias, q, m, k, BIAS, SLOTS)
                for _ in range(steps[k]):
                    next(side, None)

        side = attention()
        BODIES = N_PAIRS + 4
        LOOP = (N_PAIRS - 2 * RING - 1) // RING
        LEAD = N_PAIRS - RING * LOOP
        attending = True
        for b in range(LEAD):
            body(b // RING, b % RING, STEPS[min(b, len(STEPS) - 1)])
        for _ in side:
            pass
        attending = False
        first = LEAD // RING
        with nc.Fori(first, first + LOOP, engines=[e.engine for e in (pe, act, dve, pool)]) as i:
            for b in range(LEAD % RING, LEAD % RING + RING):
                body(i + b // RING, b % RING)
        for b in range(LEAD + RING * LOOP, BODIES):
            body(b // RING, b % RING)

        def traffic(q, m):
            qs, ms = q - 1, m
            ql, ml = q + (m + 2) // RING, (m + 2) % RING
            for h in range(2):
                if not outside(qs, ms):
                    store(qs, ms, h)
                if not outside(ql, ml) and (not isinstance(ql, int) or ql > 0):
                    load(ql, ml, h)

        LOOP_SP = (N_PAIRS - 2 - RING) // RING
        for m in range(RING):
            traffic(0, m)
        with sp.Fori(1, 1 + LOOP_SP) as i:
            for m in range(RING):
                traffic(i, m)
        for b in range(RING * (1 + LOOP_SP), BODIES):
            traffic(b // RING, b % RING)

        after(pool, result["att"])
        for m in range(RING):
            for h in range(2):
                pool.wait_ge(st[m][h], 16 * len(range(m, N_PAIRS, RING)))
        acc = sem("acc")
        for b in range(B):
            pool.dma_start(out[b, 0:LT, :], att[b * LT:(b + 1) * LT, :], accum_op=ALU.add).then_inc(acc, 16)
        pool.wait_ge(acc, 16 * B)


_INS = ['L0_attn_x', 'L0_attn_Wq', 'L0_attn_bq', 'L0_attn_Wk', 'L0_attn_Wv', 'L0_attn_bv', 'L0_attn_Wo', 'L0_attn_bo',
        'L0_attn_lna_w', 'L0_attn_lnc_w', 'L0_attn_lnd_w', 'L0_attn_Wlq', 'L0_attn_blq', 'L0_attn_Wlk', 'L0_attn_blk',
        'L0_attn_Wlv', 'L0_attn_blv', 'L0_attn_temp', 'L0_attn_threshold', 'L0_attn_factor',
        'L0_ffn_Win', 'L0_ffn_bin_', 'L0_ffn_W1', 'L0_ffn_b1', 'L0_ffn_W2', 'L0_ffn_b2', 'L0_ffn_Wout', 'L0_ffn_bout']


def kernel(**inputs):
    import numpy as _np
    import concourse.bacc as _bacc
    from concourse import mybir as _mybir
    from concourse.bass_utils import run_bass_kernel_spmd as _run

    nc = _bacc.Bacc("TRN2", target_bir_lowering=False, num_devices=1)
    arrays, args = {}, []
    for name in _INS:
        a = _np.ascontiguousarray(_np.atleast_1d(inputs[name]))
        arrays[f"in_{name}_dram"] = a
        args.append(nc.dram_tensor(f"in_{name}_dram", a.shape, _mybir.dt.from_np(a.dtype), kind="ExternalInput").ap())
    shape = inputs['L0_attn_x'].shape
    args.append(nc.dram_tensor("out_0_dram", shape, _mybir.dt.float32, kind="ExternalOutput").ap())
    residual_block(nc, *args)
    r = _run(nc, [arrays], core_ids=[0])
    return r.results[0]["out_0_dram"]
```

```python
from contextlib import ExitStack

import concourse.bass as bass
from concourse import mybir

F32 = mybir.dt.float32
F32R = mybir.dt.float32r
ACT = mybir.ActivationFunctionType
ALU = mybir.AluOpType
AX = mybir.AxisListType

P = 128
RING = 3
SLOTS = 8
EPS = 1e-5
ROUNDS = 3


def residual_block(nc, x, Wq, bq, Wk, Wv, bv, Wo, bo, lna_w, lnc_w, lnd_w, Wlq, blq, Wlk, blk, Wlv, blv,
                   temp, threshold, factor, Win, bin_, W1, b1, W2, b2, Wout, bout, out):
    B, T, D = x.shape
    M, INNER = W1.shape
    HD = Wlq.shape[0]
    H = D // HD
    DC = D // P
    TPP = 8
    BLK = TPP // 2 * P
    PAIR = 2 * BLK
    N_PAIRS = B * T // PAIR
    MH = M // 2
    HG = P // MH
    HK = INNER // HG
    assert 2 * M == P and 2 * HK == SLOTS and D == 512 and N_PAIRS >= 7

    x_v = x.rearrange("b (n p j) d -> (b n) p (j d)", p=P, j=TPP)
    out_v = out.rearrange("b (n p j) d -> (b n) p (j d)", p=P, j=TPP)

    ctx = ExitStack()
    with ctx:
        def sb(name, shape, dt=F32):
            return ctx.enter_context(nc.sbuf_tensor(name, shape, dt))

        def sem(name):
            return ctx.enter_context(nc.semaphore(name))

        pe, act, dve, pool, sp = nc.tensor, nc.scalar, nc.vector, nc.gpsimd, nc.sync

        x_sb = [sb(f"x{r}", [P, TPP * D]) for r in range(RING)]
        o_sb = [sb(f"o{r}", [P, TPP * D]) for r in range(RING)]
        xT = sb("xT", [P, DC, PAIR])
        s_full = sb("s_full", [P, BLK])
        SH = sb("SH", [P, PAIR], F32R)
        Hr = [[sb(f"H{a}{i}", [P, PAIR]) for i in range(n)] for a, n in enumerate((HK, 3))]
        G = [sb(f"G{r}", [P, PAIR], F32R) for r in range(RING)]
        stats = sb("stats", [P, TPP, 6])
        dmean = sb("dmean", [P, TPP])
        m2 = sb("m2", [P, TPP])
        dm2 = sb("dm2", [P, TPP])
        veps = sb("veps", [P, TPP])
        rstd = sb("rstd", [P, TPP])
        rwide = sb("rwide", [P, TPP // 2, 2, M])

        ident = sb("ident", [P, P])
        istack = sb("istack", [P, MH])
        spread = sb("spread", [P, 2, P], F32R)
        nhalf = sb("nhalf", [P, 16])
        win = sb("win", [P, DC, M])
        w1c = sb("w1c", [P, 2, HK])
        b1c = sb("b1c", [P, 2, HK])
        w2c = sb("w2c", [P, 2, HK])
        binc = sb("binc", [P, 2])
        b2c = sb("b2c", [P, 1])
        w2s = sb("w2s", [P, 2, HK, MH])
        wout_hi = sb("wout_hi", [P, D], F32R)
        wout_lo = sb("wout_lo", [P, D], F32R)
        bias_row = sb("bias_row", [P, D])
        ones_d = sb("ones_d", [P, P])

        def ps(name, banks=1):
            return ctx.enter_context(nc.psum_tensor(name, [P, banks * 512], F32))

        T_ps, s_ps, g_ps, o_ps, rep_ps = [ps("T0"), ps("T1")], ps("s"), ps("g"), [ps("op0"), ps("op1")], ps("rep", 2)

        ld = [[sem(f"ld{r}{h}") for h in range(2)] for r in range(RING)]
        st = [[sem(f"st{r}{h}") for h in range(2)] for r in range(RING)]
        tr_done, ev_done = sem("tr_done"), sem("ev_done")
        sc_done = sem("sc_done")
        bn_done, var_done, rstd_done = sem("bn_done"), sem("var_done"), sem("rstd_done")
        rb_done, R_done, s_done = sem("rb_done"), sem("R_done"), sem("s_done")
        sh_done, sl_done = sem("sh_done"), sem("sl_done")
        rep_done = sem("rep_done")
        relu_done, g_done = sem("relu_done"), sem("g_done")
        hi_done, lo_done = sem("hi_done"), sem("lo_done")
        op_done, xc_done, add_done = sem("op_done"), sem("xc_done"), sem("add_done")

        count = {}
        line = {id(e): sem(f"line_{n}") for e, n in ((pe, "pe"), (act, "act"), (dve, "dve"), (pool, "pool"))}

        def tick(eng, ins):
            count[id(eng)] = count.get(id(eng), 0) + 1
            ins.then_inc(line[id(eng)], 1)
            return line[id(eng)], count[id(eng)]

        def after(eng, *marks):
            for s, v in marks:
                eng.wait_ge(s, v)

        def arrive(name, eng, *copies):
            s = sem(f"in_{name}")
            with nc.allow_non_contiguous_dma(reason="small parameters"):
                for dst, src in copies:
                    eng.dma_start(dst, src).then_inc(s, 16)
            return s, 16 * len(copies)

        col = lambda v: v.rearrange("(p o) -> p o", o=1)

        HALF = TPP // 2 * D

        def rows(view, n, h):
            c = slice(h * HALF, (h + 1) * HALF)
            return view[n, :, c] if isinstance(n, int) else view[bass.ds(n, 1), :, c].rearrange("o p m -> p (o m)")

        def load(q, m, h):
            n = RING * q + m
            if not isinstance(q, int) or q > 0:
                sp.wait_ge(xc_done, SLOTS * (n - RING) + 4 * (h + 1))
            sp.dma_start(x_sb[m][:, h * HALF:(h + 1) * HALF], rows(x_v, n, h)).then_inc(ld[m][h], 16)

        LT = H
        RW = B * LT
        CR = DC * RW
        hpc = P // HD
        H2 = H // 2
        assert 2 * RW == P
        flat = lambda t: t.rearrange("p a b -> p (a b)")

        xa, lna = Hr[0][1][0:RW, 0:D], Hr[0][1][0:RW, D:2 * D]
        wo2, row1 = Hr[0][0][:, 0:D], Hr[0][0][:, D:2 * D]
        w_nat = {n: o_sb[i // 2][:, (i % 2) * DC * D:(i % 2 + 1) * DC * D].rearrange("p (c i) -> p c i", c=DC)
                 for i, n in enumerate("qkvo")}
        W_T = {"q": o_sb[2][:, 0:DC * D], "k": o_sb[2][:, DC * D:2 * DC * D],
               "v": sb("WvT", [P, DC * D])[:, :], "o": sb("WoT", [P, DC * D])[:, :]}
        W_T = {n: w.rearrange("p (c o) -> p c o", c=DC) for n, w in W_T.items()}
        NV = 5
        small = sb("small", [HD, 3 * HD + NV])
        bqc = sb("bqc", [P, DC])
        bvc = sb("bvc", [P, DC])
        scal = sb("scal", [P, 3])

        in_xa = arrive("xa", act, *[(xa[b * LT:(b + 1) * LT, :], x[b, 0:LT, :]) for b in range(B)])
        in_lna = arrive("lna", act, (lna, lna_w.partition_broadcast(RW)))
        load(0, 0, 0)
        in_win = arrive("win", sp, (win[:, :, :], Win.rearrange("(c p) m -> p c m", p=P)))
        load(0, 0, 1)
        in_w = {}

        def load_weight(n, w):
            in_w[n] = arrive(f"w{n}", sp, (w_nat[n], w.rearrange("(c p) i -> p c i", p=P)))

        load_weight("q", Wq)
        load_weight("k", Wk)
        load(0, 1, 0)
        load_weight("v", Wv)
        load_weight("o", Wo)
        load(0, 1, 1)
        in_wo2 = arrive("wo2", sp, (wo2[0:M, :], Wout), (wo2[M:P, :], Wout))
        in_rows = arrive("rows", sp, (bias_row[:, :], bout.partition_broadcast(P)), (row1, bo.partition_broadcast(P)))
        load(0, 2, 0)
        load(0, 2, 1)

        block4 = sb("block4", [P, P])
        cmask = sb("cmask", [P, RW])
        half2 = sb("half2", [P, 2])
        epsc = sb("epsc", [P, 1])
        z = tick(pool, pool.memset(ident[:, :], 0.0))
        after(pool, z)
        mk_ident = tick(pool, pool.affine_select(out=ident[:, :], in_=ident[:, :], compare_op=ALU.not_equal, fill=1.0,
                                                 base=0, pattern=[[-1, P]], channel_multiplier=1))
        mk_ones = tick(pool, pool.memset(ones_d[:, :], 1.0))
        tick(pool, pool.memset(nhalf[:, :], -0.5))
        tick(pool, pool.memset(epsc[:, :], EPS))
        tick(pool, pool.memset(cmask[:, :], 0.0))
        tick(pool, pool.memset(half2[:, :], 1.0))
        z = tick(pool, pool.memset(block4[:, :], 1.0))
        after(pool, z)

        def band(ap, width, groups, inner, fill):
            after(pool, tick(pool, pool.affine_select(out=ap, in_=ap, compare_op=ALU.is_ge, fill=fill, base=0,
                                                      pattern=[[-width, groups], [0, inner]], channel_multiplier=1)))
            t = tick(pool, pool.affine_select(out=ap, in_=ap, compare_op=ALU.is_ge, fill=fill, base=width - 1,
                                              pattern=[[width, groups], [0, inner]], channel_multiplier=-1))
            after(pool, t)
            return t

        band(block4[:, :].rearrange("p (g i) -> p g i", g=hpc), HD, hpc, HD, 0.0)
        band(half2[:, :].rearrange("p (g i) -> p g i", g=2), P // 2, 2, 1, 0.0)
        for f in range(2):
            mk_pool = band(cmask[f * RW:(f + 1) * RW, :].rearrange("p (g i) -> p g i", g=B), LT, B, LT, -1e30)

        wmean = sb("wmean", [P, M])
        after(pe, mk_ident)

        tmp = {n: sb(n, shape) for n, shape in (("isum", [P, M]), ("wb", [P, 2, HK]))}

        def centre_win():
            after(pe, mk_ones, in_win)
            for c in range(DC):
                mm = pe.matmul(g_ps[:, 0:M], ones_d[:, :], win[:, c, :], start=(c == 0), stop=(c == DC - 1))
            t = tick(pe, mm)
            after(dve, t)
            t = tick(dve, dve.tensor_scalar(wmean[:, :], g_ps[:, 0:M], 1.0 / D, None, ALU.mult))
            after(dve, t)
            t = tick(dve, dve.tensor_tensor(win[:, :, :], win[:, :, :], wmean[:, :].unsqueeze(1).to_broadcast([P, DC, M]), ALU.subtract))
            made["win"] = t
            yield

        def constants():
            after(dve, mk_ident)
            a = tick(dve, dve.tensor_tensor(tmp["isum"][:, :], ident[:, 0:M], ident[:, M:P], ALU.add))
            after(dve, a)
            a = tick(dve, dve.tensor_tensor(istack[:, :], tmp["isum"][:, 0:MH], tmp["isum"][:, MH:M], ALU.add))
            for half in range(2):
                a = tick(dve, dve.tensor_copy(spread[:, half, :].rearrange("p (g m) -> p g m", g=HG),
                                              tmp["isum"][:, half * MH:(half + 1) * MH].unsqueeze(1).to_broadcast([P, HG, MH])))
            made["spread"] = a
            yield
            after(dve, a, made["ffn"])
            a = tick(dve, dve.tensor_tensor(tmp["wb"][:, :, :], w1c[:, :, :], binc[:, :].unsqueeze(2).to_broadcast([P, 2, HK]), ALU.mult))
            after(dve, a)
            made["relu"] = tick(dve, dve.tensor_tensor(b1c[:, :, :], tmp["wb"][:, :, :], b1c[:, :, :], ALU.add))
            for half in range(2):
                for k in range(HK):
                    a = tick(dve, dve.tensor_scalar(w2s[:, half, k, :], istack[:, :], w2c[:, half, k:k + 1], None, ALU.mult))
            made["w2s"] = a
            yield
            after(dve, in_wo2, in_rows)
            a = tick(dve, dve.tensor_copy(wout_hi[:, :], wo2))
            b = tick(dve, dve.tensor_tensor(bias_row[:, :], bias_row[:, :], row1, ALU.add))
            after(dve, a)
            a = tick(dve, dve.tensor_tensor(wout_lo[:, :], wo2, wout_hi[:, :].bitcast(F32), ALU.subtract))
            made["bias"], made["wout"] = b, a
            yield

        SM = float(HD) ** -0.5
        QS = float(HD) ** -0.25
        mv = sb("mv", [RW, 8])
        ms = sb("ms", [RW, 16])
        xn_all = sb("xn", [P, D])
        xn = xn_all[0:RW, :]
        xnT = sb("xnT", [P, DC, RW])
        qkn = sb("qkn", [P, D])
        sq = sb("vn", [P, D])
        vn = sq[:, 0:D // 2]
        qT = sb("qT", [P, DC, RW])
        kT = sb("kT", [P, CR])
        vT = sb("vT", [P, DC, 2, RW])
        bqs = sb("bqs", [P, DC])
        tile4 = sb("tile4", [HD, P])
        rep = sb("repw", [P, 3 * HD + NV])
        centre = sb("centre", [P, P])
        avg = sb("avg", [P, P])
        nat = sb("nat", [P, 3, P])
        bd = sb("bd", [P, 4, P])
        var16 = sb("var16", [P, 4 * hpc])
        rstd16 = sb("rstd16", [P, 4 * hpc])
        bqk = sb("bqk", [P, 2])
        hmask = sb("hmask", [P, hpc])
        tt = sb("tt", [P, 4, ROUNDS])
        wq_it = sb("wq_it", [P, ROUNDS])
        qk = sb("qk", [P, 2, CR])
        over_v = flat(W_T["v"])
        kbd = over_v[:, 0:hpc * CR].rearrange("p (c h r) -> p c h r", c=DC, h=hpc)
        lg = over_v[:, hpc * CR:(hpc + 2) * CR].rearrange("p (h r) -> p h r", r=RW)
        AT = over_v[:, (hpc + 2) * CR:(hpc + 4) * CR].rearrange("p (a b) -> p a b", a=4)
        Vbd = qkn[:, :].rearrange("p (g a d) -> p g a d", a=2, d=HD)
        red = sb("red", [P, 3, H2])
        ai = [xn_all[:, 0:CR], xn_all[:, CR:2 * CR], flat(xnT[:, :, :])]
        dsum = sb("dsum", [P, 8])
        att = vn
        chunks = lambda t: t.rearrange("p (c r) -> p c r", c=DC)
        wide = lambda c: c.unsqueeze(2).to_broadcast([P, DC, RW])
        heads = lambda t: t.rearrange("p (h d) -> p h d", h=hpc)
        heads8 = lambda t: t.rearrange("p (h r) -> p h r", r=RW)
        over8 = lambda t: t.unsqueeze(2).to_broadcast([P, H2, RW])
        A_ps = o_ps[1]
        made = {}

        def row_norm(src, dst, marks):
            after(dve, *marks)
            a = tick(dve, dve.bn_stats(mv[:, 0:6], src))
            after(dve, a)
            a = tick(dve, dve.bn_aggr(ms[:, 0:2], mv[:, 0:6]))
            after(dve, a)
            a = tick(dve, dve.tensor_scalar(ms[:, 2:3], ms[:, 1:2], EPS, None, ALU.add))
            after(pool, a)
            a = tick(pool, pool.tensor_tensor(ms[:, 3:4], ms[:, 2:3], nhalf[0:RW, 0:1], ALU.pow))
            yield
            after(dve, a)
            yield tick(dve, dve.tensor_scalar(dst, src, ms[:, 0:1], ms[:, 3:4], ALU.subtract, ALU.mult))

        def attention():
            yield from centre_win()
            a = None
            for src, dst in ((xa, xn[:, :]), (xn[:, :], xa)):
                for mark in row_norm(src, dst, (a or in_xa,)):
                    a = mark or a
                    yield
            after(dve, a, in_lna)
            xn_done = tick(dve, dve.tensor_tensor(xn[:, :], xa, lna, ALU.mult))
            made["xn"] = xn_done
            in_small = arrive(
                "small", act,
                *[(small[:, i * HD:(i + 1) * HD], w) for i, w in enumerate((Wlq, Wlk, Wlv))],
                *[(small[:, 3 * HD + i:3 * HD + i + 1], col(v)) for i, v in enumerate((blq, blk, blv, lnc_w, lnd_w))])
            in_bq = arrive("bq", act, (bqc[:, :], bq.rearrange("(c p) -> p c", p=P)), (bvc[:, :], bv.rearrange("(c p) -> p c", p=P)))
            in_scal = arrive("scal", act, *[(scal[:, i:i + 1], v.partition_broadcast(P)) for i, v in enumerate((temp, threshold, factor))])
            by_g = lambda w, a: w[a * MH:(a + 1) * MH, :].rearrange("m (g h) -> g m h", g=HG)
            made["ffn"] = arrive(
                "ffn", pool,
                *[(dst[:, a, :], by_g(src, a)) for dst, src in ((w1c, W1), (b1c, b1), (w2c, W2)) for a in range(2)],
                *[(binc[g * MH:(g + 1) * MH, :], bin_.rearrange("(a m) -> m a", a=2)) for g in range(HG)],
                *[(b2c[f * M:(f + 1) * M, :], col(b2)) for f in range(2)])

            banks = [rep_ps[:, 0:D], rep_ps[:, D:2 * D], o_ps[0][:, :]]
            NB = len(banks)
            evacs = []

            def turn(n):
                after(pe, in_w[n])
                for ic in range(DC):
                    u = len(evacs)
                    if u >= NB:
                        after(pe, evacs[u - NB])
                    for oc in range(DC):
                        mm = pe.transpose(banks[u % NB][:, oc * P:(oc + 1) * P], w_nat[n][:, oc, ic * P:(ic + 1) * P], ident[:, :])
                    t = tick(pe, mm)
                    if u % 2:
                        after(act, t)
                        evacs.append(tick(act, act.activation(W_T[n][:, ic, :], banks[u % NB], ACT.Copy)))
                    else:
                        after(dve, t)
                        evacs.append(tick(dve, dve.tensor_copy(W_T[n][:, ic, :], banks[u % NB])))
                    if ic % 2:
                        yield

            after(pe, xn_done)
            for c in range(DC):
                mm = pe.transpose(A_ps[:, c * RW:(c + 1) * RW], xn[:, c * P:(c + 1) * P], ident[0:RW, 0:RW])
            a = tick(pe, mm)
            after(act, a)
            xnT_done = tick(act, act.activation(flat(xnT[:, :, :]), A_ps[:, 0:CR], ACT.Copy))
            yield
            yield from turn("q")
            yield from turn("k")
            made["k turned"] = evacs[-2:]
            yield from turn("v")
            yield from turn("o")
            made["weights turned"] = evacs[-4:]
            yield
            yield from constants()
            after(pe, xnT_done)
            for ic in range(DC):
                for i, n in enumerate("qk"):
                    mm = pe.matmul(A_ps[i * RW:(i + 1) * RW, :], xnT[:, ic, :], W_T[n][:, ic, :], start=(ic == 0), stop=(ic == DC - 1))
            a = tick(pe, mm)
            yield
            after(act, a)
            a = tick(act, act.activation(qkn[:, :], A_ps[:, :], ACT.Copy, scale=QS))
            yield
            after(pe, a)
            for ic in range(DC):
                for f in range(2):
                    mm = pe.matmul(A_ps[f * RW:(f + 1) * RW, 0:D // 2], xnT[:, ic, :], W_T["v"][:, ic, f * D // 2:(f + 1) * D // 2],
                                   start=(ic == 0), stop=(ic == DC - 1))
            b = tick(pe, mm)
            yield
            after(act, b)
            b = tick(act, act.activation(vn[:, :], A_ps[:, 0:D // 2], ACT.Copy))
            yield
            after(pe, b)
            made["q, k, v"] = b
            yield
            for c in range(DC):
                mm = pe.transpose(A_ps[:, c * P:(c + 1) * P], qkn[:, c * P:(c + 1) * P], ident[:, :])
            a = tick(pe, mm)
            after(dve, in_bq)
            t = tick(dve, dve.tensor_scalar(bqs[:, :], bqc[:, :], QS, None, ALU.mult))
            yield
            after(dve, t, a)
            qk_ps = A_ps[:, :].rearrange("p (c a r) -> p c a r", c=DC, a=2)
            tick(dve, dve.tensor_tensor(qT[:, :, :], qk_ps[:, :, 0, :], wide(bqs[:, :]), ALU.add))
            a = tick(dve, dve.tensor_copy(chunks(kT[:, :]), qk_ps[:, :, 1, :]))
            yield
            after(pe, a)
            for c in range(DC // 2):
                mm = pe.transpose(A_ps[:, c * P:(c + 1) * P], vn[:, c * P:(c + 1) * P], ident[:, :])
            a = tick(pe, mm)
            yield
            after(dve, a)
            qkv_done = tick(dve, dve.tensor_tensor(
                vT[:, :, 0, :].rearrange("p (f c) r -> p f c r", f=2), A_ps[:, 0:CR].rearrange("p (c f r) -> p f c r", f=2, r=RW),
                bvc[:, :].rearrange("p (f c) -> p f c", f=2).unsqueeze(3).to_broadcast([P, 2, DC // 2, RW]), ALU.add))
            yield

            after(dve, mk_pool)
            t = tick(dve, dve.tensor_copy(tile4[:, :].rearrange("p (h d) -> p h d", h=hpc),
                                          ident[0:HD, 0:HD].unsqueeze(1).to_broadcast([HD, hpc, HD])))
            a = tick(dve, dve.tensor_scalar(avg[:, :], block4[:, :], 1.0 / HD, None, ALU.mult))
            after(dve, a)
            tick(dve, dve.tensor_tensor(centre[:, :], ident[:, :], avg[:, :], ALU.subtract))
            yield
            after(pe, t, qkv_done, in_small)
            t = tick(pe, pe.matmul(A_ps[:, 0:3 * HD + NV], tile4[:, :], small[:, :], start=True, stop=True))
            yield
            after(dve, t)
            t = tick(dve, dve.tensor_copy(rep[:, :], A_ps[:, 0:3 * HD + NV]))
            after(dve, t)
            for i in range(3):
                t = tick(dve, dve.tensor_tensor(heads(nat[:, i, :]), rep[:, i * HD:(i + 1) * HD].unsqueeze(1).to_broadcast([P, hpc, HD]),
                                                heads(block4[:, :]), ALU.mult))
            yield
            after(pe, t)
            for j, (i, rhs) in enumerate(((0, centre), (1, centre), (1, ident), (2, ident))):
                mm = pe.matmul(A_ps[:, j * P:(j + 1) * P], nat[:, i, :], rhs[:, :], start=True, stop=True)
            t = tick(pe, mm)
            yield
            after(dve, t)
            t = tick(dve, dve.tensor_copy(flat(bd[:, :, :]), A_ps[:, :]))
            yield
            after(pe, t)
            t = tick(pe, pe.matmul(A_ps[:, 0:2], centre[:, :], rep[:, 3 * HD:3 * HD + 2], start=True, stop=True))
            yield
            after(dve, t, in_scal)
            a = tick(dve, dve.tensor_copy(bqk[:, :], A_ps[:, 0:2]))
            blkv = rep[:, 3 * HD + 1:3 * HD + 3]
            tick(dve, dve.tensor_scalar(hmask[:, :], block4[:, ::HD], rep[:, 3 * HD + 4:3 * HD + 5], None, ALU.mult))
            for it in range(ROUNDS):
                t = tick(dve, dve.tensor_scalar(tt[:, 0, it:it + 1], scal[:, 0:1], 0.005 * it, None, ALU.add))
            after(dve, t)
            tick(dve, dve.tensor_scalar(tt[:, 1, :], tt[:, 0, :], 0.0, None, ALU.is_gt))
            t = tick(dve, dve.tensor_scalar(tt[:, 2, :], tt[:, 0, :], 1.0, None, ALU.subtract))
            after(dve, t)
            t = tick(dve, dve.tensor_tensor(tt[:, 2, :], tt[:, 2, :], tt[:, 1, :], ALU.mult))
            after(dve, t)
            t = tick(dve, dve.tensor_scalar(tt[:, 2, :], tt[:, 2, :], 1.0, None, ALU.add))
            yield
            after(pool, t)
            t = tick(pool, pool.tensor_tensor(tt[:, 3, :], tt[:, 2, :], nhalf[:, 0:ROUNDS], ALU.pow))
            temp_mark, free = t, (a,)
            for it in range(ROUNDS):
                after(pe, *free)
                pe.matmul(A_ps[:, 0:CR], bd[:, 0, :], flat(qT[:, :, :]), start=True, stop=True)
                a = tick(pe, pe.matmul(A_ps[:, CR:2 * CR], bd[:, 1, :], kT[:, :], start=True, stop=True))
                yield
                after(dve, a)
                qk_done = tick(dve, dve.tensor_tensor(qk[:, :, :], A_ps[:, :].rearrange("p (a c) -> p a c", a=2),
                                                      bqk[:, :].unsqueeze(2).to_broadcast([P, 2, CR]), ALU.add))
                yield
                after(pe, qk_done)
                pe.matmul(A_ps[:, 0:CR], bd[:, 2, :], kT[:, :], start=True, stop=True)
                a = tick(pe, pe.matmul(A_ps[:, CR:2 * CR], bd[:, 3, :], vT[:, :, 0, :], start=True, stop=True))
                after(act, qk_done)
                sq_done = tick(act, act.activation(sq[:, :], flat(qk[:, :, :]), ACT.Square))
                yield
                after(dve, a)
                tick(dve, dve.tensor_scalar(kT[:, :], A_ps[:, 0:CR], blkv[:, 0:1], None, ALU.add))
                a = tick(dve, dve.tensor_scalar(vT[:, :, :, :], chunks(A_ps[:, CR:2 * CR]).unsqueeze(2).to_broadcast([P, DC, 2, RW]),
                                                blkv[:, 1:2], None, ALU.add))
                yield
                after(pe, a, sq_done)
                for g in range(4):
                    mm = pe.matmul(A_ps[:, g * hpc:(g + 1) * hpc], sq[:, g * P:(g + 1) * P], avg[:, ::HD], start=True, stop=True)
                a = tick(pe, mm)
                yield
                after(act, a)
                a = tick(act, act.activation(var16[:, :], A_ps[:, 0:4 * hpc], ACT.Identity, bias=epsc[:, 0:1]))
                after(pool, a)
                r_mark = tick(pool, pool.tensor_tensor(rstd16[:, :], var16[:, :], nhalf[:, 0:4 * hpc], ALU.pow))
                yield
                after(pe, a)
                for c in range(DC):
                    mm = pe.transpose(A_ps[:, c * P:(c + 1) * P], vT[:, c, :, :].rearrange("p a r -> p (a r)"), ident[:, :])
                v_mark = tick(pe, mm)
                yield
                after(dve, v_mark)
                v_mark = tick(dve, dve.tensor_tensor(Vbd[:, :, :, :], A_ps[:, :].rearrange("p (g a d) -> p g a d", a=2, d=HD),
                                                     half2[:, :].unsqueeze(1).unsqueeze(3).to_broadcast([P, H2, 2, HD]), ALU.mult))
                yield
                yield
                after(act, r_mark)
                a = tick(act, act.activation(sq[:, :].rearrange("p (g d) -> p g d", d=HD),
                                             rstd16[:, :].unsqueeze(2).to_broadcast([P, 4 * hpc, HD]), ACT.Copy))
                yield
                after(pe, a, v_mark)
                for g in range(4):
                    mm = pe.transpose(A_ps[:, g * P:(g + 1) * P], sq[:, g * P:(g + 1) * P], ident[:, :])
                a = tick(pe, mm)
                yield
                after(dve, a)
                a = tick(dve, dve.tensor_tensor(flat(qk[:, :, :]), flat(qk[:, :, :]), A_ps[:, :], ALU.mult))
                yield
                after(dve, a)
                tick(dve, dve.tensor_tensor(kbd[:, :, :, :], chunks(qk[:, 1, :]).unsqueeze(2).to_broadcast([P, DC, hpc, RW]),
                                            hmask[:, :].unsqueeze(1).unsqueeze(3).to_broadcast([P, DC, hpc, RW]), ALU.mult))
                if it == 0:
                    after(dve, temp_mark)
                    after(dve, tick(dve, dve.tensor_scalar(wq_it[:, :], tt[:, 3, :], rep[:, 3 * HD + 3:3 * HD + 4], None, ALU.mult)))
                a = tick(dve, dve.tensor_scalar(qk[:, 0, :], qk[:, 0, :], wq_it[:, it:it + 1], None, ALU.mult))
                yield
                after(pe, a)
                for w in range(2):
                    for f in range(2):
                        c = 2 * f + w
                        mm = pe.matmul(A_ps[f * RW:(f + 1) * RW, w * CR:(w + 1) * CR], qk[:, 0, c * RW:(c + 1) * RW],
                                       kbd[:, c, :, :], start=True, stop=True)
                a = tick(pe, mm)
                yield
                after(dve, a)
                a = tick(dve, dve.tensor_tensor(lg[:, :, :], heads8(A_ps[:, :]), cmask[:, :].unsqueeze(1).to_broadcast([P, H2, RW]), ALU.add))
                yield
                after(dve, a)
                a = tick(dve, dve.tensor_reduce(red[:, 0, :], lg[:, :, :], AX.X, ALU.max))
                after(pool, a)
                a = tick(pool, pool.tensor_tensor(lg[:, :, :], lg[:, :, :], over8(red[:, 0, :]), ALU.subtract))
                yield
                yield
                after(act, a)
                a = tick(act, act.activation(flat(lg[:, :, :]), flat(lg[:, :, :]), ACT.Exp, scale=SM))
                yield
                after(dve, a)
                a = tick(dve, dve.tensor_reduce(red[:, 1, :], lg[:, :, :], AX.X, ALU.add))
                after(dve, a)
                a = tick(dve, dve.reciprocal(red[:, 2, :], red[:, 1, :]))
                yield
                after(dve, a)
                a = tick(dve, dve.tensor_tensor(lg[:, :, :], lg[:, :, :], over8(red[:, 2, :]), ALU.mult))
                yield
                after(pe, a)
                for j in range(4):
                    mm = pe.transpose(A_ps[:, j * P:(j + 1) * P], lg[:, 2 * j:2 * j + 2, :].rearrange("p a b -> p (a b)"), ident[:, :])
                a = tick(pe, mm)
                yield
                after(act, a)
                a = tick(act, act.activation(flat(AT[:, :, :]), A_ps[:, :], ACT.Copy))
                yield
                after(pe, a, v_mark)
                for g in range(H2):
                    f, j = g // 4, g % 4
                    mm = pe.matmul(A_ps[(g % 2) * RW:(g % 2 + 1) * RW, (g // 2) * RW:(g // 2 + 1) * RW],
                                   Vbd[:, g, :, :].rearrange("p a d -> p (a d)"), AT[:, j, f * RW:(f + 1) * RW], start=True, stop=True)
                a = tick(pe, mm)
                yield
                after(dve, a)
                t = tick(dve, dve.tensor_copy(ai[it][:, :], A_ps[:, 0:CR]))
                free = (tick(dve, dve.tensor_tensor(flat(qT[:, :, :]), flat(qT[:, :, :]), A_ps[:, 0:CR], ALU.add)),)
                yield

            after(dve, t)
            a = tick(dve, dve.tensor_tensor(sq[:, 0:CR], ai[1][:, :], ai[0][:, :], ALU.subtract))
            yield
            after(act, a)
            a = tick(act, act.activation(sq[:, CR:2 * CR], sq[:, 0:CR], ACT.Abs, accum_out=dsum[:, 0:1]))
            yield
            after(pe, a, *free)
            a = tick(pe, pe.matmul(A_ps[:, 0:1], ones_d[:, :], dsum[:, 0:1], start=True, stop=True))
            yield
            after(dve, a)
            a = tick(dve, dve.tensor_scalar(dsum[:, 1:2], A_ps[:, 0:1], 1.0 / (B * H * T * HD), None, ALU.mult))
            after(dve, a)
            a = tick(dve, dve.tensor_scalar(dsum[:, 2:3], dsum[:, 1:2], scal[:, 2:3], scal[:, 1:2], ALU.mult, ALU.add))
            after(dve, a)
            a = tick(dve, dve.tensor_tensor(dsum[:, 3:4], dsum[:, 1:2], dsum[:, 2:3], ALU.is_lt))
            after(dve, a)
            a = tick(dve, dve.tensor_scalar(dsum[:, 4:5], dsum[:, 3:4], -1.0, 1.0, ALU.mult, ALU.add))
            after(dve, a)
            a = tick(dve, dve.tensor_scalar(ai[2][:, :], ai[2][:, :], dsum[:, 4:5], None, ALU.mult))
            after(dve, a)
            a = tick(dve, dve.scalar_tensor_tensor(ai[1][:, :], ai[1][:, :], dsum[:, 3:4], ai[2][:, :], ALU.mult, ALU.add))
            yield
            after(pe, a)
            for c in range(DC):
                for f in range(2):
                    mm = pe.matmul(A_ps[f * RW:(f + 1) * RW, 0:D // 2], ai[1][:, c * RW:(c + 1) * RW],
                                   W_T["o"][:, c, f * D // 2:(f + 1) * D // 2], start=(c == 0), stop=(c == DC - 1))
            a = tick(pe, mm)
            yield
            after(act, a)
            made["att"] = tick(act, act.activation(att[:, :], A_ps[:, 0:D // 2], ACT.Copy))
            after(pe, made["att"])

        def at(q, m):
            return RING * q + m

        def outside(q, m):
            return isinstance(q, int) and not 0 <= at(q, m) < N_PAIRS

        def positive(v):
            return not isinstance(v, int) or v > 0

        def wait(eng, s, v):
            if positive(v):
                eng.wait_ge(s, v)

        def need(eng, pair, n, *names):
            if isinstance(n, int) and n == pair:
                for name in names:
                    while name not in made:
                        next(side)
                    r = made[name]
                    after(eng, *(r if isinstance(r, list) else [r]))

        def transpose(q, m, k):
            c, b = k // 2, k % 2
            n = at(q, m)
            if k < 2:
                wait(pe, ld[m][k], 16 * (q + 1))
            wait(pe, ev_done, SLOTS * n + k - 1)
            for j in range(4):
                col0 = (4 * b + j) * D + c * P
                mm = pe.transpose(T_ps[k % 2][:, j * P:(j + 1) * P], x_sb[m][:, col0:col0 + P], ident[:, :])
            mm.then_inc(tr_done, 1)

        def evacuate(q, m, k):
            c, b = k // 2, k % 2
            n = at(q, m)
            wait(act, tr_done, SLOTS * n + k + 1)
            wait(act, sc_done, 4 * (n - 1) + c + 1)
            act.activation(xT[:, c, b * BLK:(b + 1) * BLK], T_ps[k % 2][:, :], ACT.Copy).then_inc(ev_done, 1)

        def s_product(q, m, c):
            n = at(q, m)
            if c == 0:
                need(pe, 0, n, "win")
            wait(pe, ev_done, SLOTS * n + 2 * c + 2)
            if c == 0:
                wait(pe, s_done, n)
            for b in range(2):
                mm = pe.matmul(s_ps[b * M:(b + 1) * M, :], win[:, c, :], xT[:, c, b * BLK:(b + 1) * BLK],
                               start=(c == 0), stop=(c == DC - 1))
            mm.then_inc(sc_done, 1)

        def statistics(q, m, j):
            n = at(q, m)
            if j % 4 == 0:
                wait(dve, ld[m][j // 4], 16 * (q + 1))
            dve.bn_stats(stats[:, j, :], x_sb[m][:, j * D:(j + 1) * D]).then_inc(bn_done, 1)

        def variance(q, m):
            n = at(q, m)
            base = (TPP + 3) * n + TPP
            wait(dve, bn_done, base)
            dve.tensor_tensor(dmean[:, :], stats[:, :, 1], stats[:, :, 4], ALU.subtract).then_inc(bn_done, 1)
            dve.scalar_tensor_tensor(m2[:, :], stats[:, :, 2], D * EPS, stats[:, :, 5], ALU.add, ALU.add).then_inc(bn_done, 1)
            wait(dve, bn_done, base + 1)
            dve.scalar_tensor_tensor(dm2[:, :], dmean[:, :], 0.25, dmean[:, :], ALU.mult, ALU.mult).then_inc(bn_done, 1)
            wait(dve, bn_done, base + 3)
            dve.scalar_tensor_tensor(veps[:, :], m2[:, :], 1.0 / D, dm2[:, :], ALU.mult, ALU.add).then_inc(var_done, 1)

        def inv_std(q, m):
            n = at(q, m)
            wait(pool, var_done, n + 1)
            pool.tensor_tensor(rstd[:, :], veps[:, :], nhalf[:, 0:TPP], ALU.pow).then_inc(rstd_done, 1)
            wait(pool, rstd_done, 2 * n + 1)
            pool.tensor_tensor(rwide[:, :, :, :], rstd[:, :].rearrange("p (b j) -> p j b", b=2).unsqueeze(3)
                               .to_broadcast([P, TPP // 2, 2, M]),
                               ones_d[:, :].rearrange("p (b m) -> p b m", b=2).unsqueeze(1).to_broadcast([P, TPP // 2, 2, M]),
                               ALU.mult).then_inc(rstd_done, 1)

        def spread_rstd(q, m):
            n = at(q, m)
            wait(pe, rstd_done, 2 * n + 2)
            wait(pe, lo_done, 2 * (n - 1))
            for j in range(4):
                mm = pe.transpose(g_ps[:, j * P:(j + 1) * P], rwide[:, j, :, :].rearrange("p b m -> p (b m)"), ident[:, :])
            mm.then_inc(rb_done, 1)

        def copy_rstd(q, m):
            n = at(q, m)
            wait(act, rb_done, n + 1)
            wait(act, sl_done, 2 * n)
            act.activation(s_full[:, :], g_ps[:, :], ACT.Copy).then_inc(R_done, 1)

        def scale_s(q, m):
            n = at(q, m)
            wait(dve, sc_done, 4 * n + 4)
            wait(dve, R_done, n + 1)
            dve.tensor_tensor(s_full[:, :], s_ps[:, :], s_full[:, :], ALU.mult).then_inc(s_done, 1)

        def halves(b):
            return slice(b * M, (b + 1) * M), slice((1 - b) * M, (2 - b) * M), slice(b * BLK, (b + 1) * BLK)

        def s_high(q, m):
            n = at(q, m)
            wait(act, s_done, n + 1)
            wait(act, rep_done, 2 * n)
            for b in range(2):
                own, _, cols = halves(b)
                act.activation(SH[own, cols], s_full[own, :], ACT.Copy).then_inc(sh_done, 1)

        def s_low(q, m):
            n = at(q, m)
            for b in range(2):
                own, other, cols = halves(b)
                wait(dve, sh_done, 2 * n + b + 1)
                dve.tensor_tensor(SH[other, cols], s_full[own, :], SH[own, cols].bitcast(F32), ALU.subtract).then_inc(sl_done, 1)

        def replicate(q, m, half):
            n = at(q, m)
            need(pe, 0, n, "weights turned", "spread")
            if half == 0:
                wait(pe, sl_done, 2 * n + 2)
            wait(pe, relu_done, SLOTS * n + HK * half)
            for b in range(2):
                cols = slice(b * BLK, (b + 1) * BLK)
                mm = pe.matmul(rep_ps[:, cols], spread[:, half, :], SH[:, cols], start=True, stop=True)
            mm.then_inc(rep_done, 1)

        def relu(q, m, r):
            n, half, k = at(q, m), r // HK, r % HK
            if k == 0:
                need(act, 0, n, "xn", "relu", "wout")
                wait(act, rep_done, 2 * n + half + 1)
            if half == 0:
                wait(act, g_done, HK * (n - 1) + k + 1)
            else:
                wait(act, g_done, HK * (n - 1) + (HK, k + 1, k + 1, HK + 1)[k])
            act.activation(Hr[half][k % len(Hr[half])][:, :], rep_ps[:, :], ACT.Relu,
                           bias=b1c[:, half, k:k + 1], scale=w1c[:, half, k:k + 1]).then_inc(relu_done, 1)

        def sum_h(q, m, k):
            n = at(q, m)
            wait(pe, relu_done, SLOTS * n + HK + k + 1)
            if k == 0:
                need(pe, 0, n, "w2s")
                if isinstance(n, int) and n == N_PAIRS - 1:
                    wait(pe, lo_done, 2 * n)
                else:
                    wait(pe, R_done, n + 2)
            for half in range(2):
                for b in range(2):
                    at0 = b * M + half * MH
                    mm = pe.matmul(g_ps[at0:at0 + MH, :], w2s[:, half, k, :],
                                   Hr[half][k % len(Hr[half])][:, b * BLK:(b + 1) * BLK], start=(k == 0), stop=(k == HK - 1),
                                   tile_position=(0, at0))
            mm.then_inc(g_done, 1)

        def g_high(q, m):
            n = at(q, m)
            wait(act, g_done, HK * n + HK)
            for b in range(2):
                own, _, cols = halves(b)
                act.activation(G[m][own, cols], g_ps[own, :], ACT.Identity, bias=b2c[own, 0:1]).then_inc(hi_done, 1)

        def g_low(q, m):
            n = at(q, m)
            for b in range(2):
                own, other, cols = halves(b)
                wait(dve, hi_done, 2 * n + b + 1)
                dve.scalar_tensor_tensor(G[m][other, cols], g_ps[own, :], b2c[own, 0:1], G[m][own, cols].bitcast(F32),
                                         ALU.add, ALU.subtract).then_inc(lo_done, 1)

        def product_bank(j):
            return o_ps[0 if attending else j % 2][:, :]

        def project(q, m, j):
            n = at(q, m)
            if j == 0:
                need(pe, 0, n, "wout")
                wait(pe, lo_done, 2 * n + 2)
            wait(pe, add_done, SLOTS * n + j - (0 if attending else 1))
            bank = product_bank(j)
            for part in (wout_hi, wout_lo):
                mm = pe.matmul(bank, G[m][:, j * P:(j + 1) * P], part[:, :], start=(part is wout_hi), stop=(part is wout_lo))
            mm.then_inc(op_done, 1)

        def add_bias(q, m, j):
            n = at(q, m)
            if j == 0:
                need(pool, m, n, ("k turned", "weights turned", "q, k, v")[m], "bias")
            if j % 4 == 0:
                wait(pool, ld[m][j // 4], 16 * (q + 1))
                wait(pool, st[m][j // 4], 16 * q)
                wait(pool, tr_done, SLOTS * n + SLOTS)
            c = slice(j * D, (j + 1) * D)
            pool.tensor_tensor(o_sb[m][:, c], x_sb[m][:, c], bias_row[:, :], ALU.add).then_inc(xc_done, 1)

        def add(q, m, j):
            n = at(q, m)
            wait(dve, op_done, SLOTS * n + j + 1)
            wait(dve, xc_done, SLOTS * n + j + 1)
            c = slice(j * D, (j + 1) * D)
            dve.tensor_tensor(o_sb[m][:, c], o_sb[m][:, c], product_bank(j), ALU.add).then_inc(add_done, 1)

        def store(q, m, h):
            n = at(q, m)
            wait(sp, add_done, SLOTS * n + 4 * (h + 1))
            sp.dma_start(rows(out_v, n, h), o_sb[m][:, h * HALF:(h + 1) * HALF]).then_inc(st[m][h], 16)

        S_PRODUCT = (2, 7, 8, 9)
        STATISTICS = ((), (0, 1), (2,), (3, 4), (5,), (6, 7), (), ())
        VARIANCE, INV_STD, SPREAD, COPY_R, SCALE, HIGH, LOW = 5, 6, 9, 9, 10, 11, 12
        REPLICATE, RELU, SUM_H, G_HIGH, G_LOW, PROJECT, ADD, BIAS = (13, 17), 13, 19, 23, 24, 25, 26, 10

        def run(stage, q, m, k, first, width=1):
            for back in range(5):
                j = k + SLOTS * back - first
                if 0 <= j < width:
                    mm = m - back
                    qq = q + mm // RING
                    if not outside(qq, mm % RING):
                        stage(qq, mm % RING, *((j,) if width > 1 else ()))

        def body(q, m):
            for k in range(SLOTS):
                run(transpose, q, m, k, 0, SLOTS)
                run(spread_rstd, q, m, k, SPREAD)
                run(s_high, q, m, k, HIGH)
                run(evacuate, q, m, k, 0, SLOTS)
                run(copy_rstd, q, m, k, COPY_R)
                run(add, q, m, k, ADD, SLOTS)
                run(scale_s, q, m, k, SCALE)
                run(s_low, q, m, k, LOW)
                run(g_low, q, m, k, G_LOW)
                run(inv_std, q, m, k, INV_STD)
                next(side, None)
                run(project, q, m, k, PROJECT, SLOTS)
                for half in range(2):
                    run(lambda a, b: replicate(a, b, half), q, m, k, REPLICATE[half])
                run(sum_h, q, m, k, SUM_H, HK)
                for c, slot in enumerate(S_PRODUCT):
                    run(lambda a, b: s_product(a, b, c), q, m, k, slot)
                run(g_high, q, m, k, G_HIGH)
                run(relu, q, m, k, RELU, 2 * HK)
                for j in STATISTICS[k]:
                    run(lambda a, b: statistics(a, b, j), q, m, k, k)
                run(variance, q, m, k, VARIANCE)
                run(add_bias, q, m, k, BIAS, SLOTS)
                next(side, None)

        side = attention()
        BODIES = N_PAIRS + 4
        LOOP = (N_PAIRS - 2 * RING - 1) // RING
        LEAD = N_PAIRS - RING * LOOP
        attending = True
        for b in range(LEAD):
            body(b // RING, b % RING)
            attending = "att" not in made
        assert not attending
        first = LEAD // RING
        with nc.Fori(first, first + LOOP, engines=[e.engine for e in (pe, act, dve, pool)]) as i:
            for b in range(LEAD % RING, LEAD % RING + RING):
                body(i + b // RING, b % RING)
        for b in range(LEAD + RING * LOOP, BODIES):
            body(b // RING, b % RING)

        def traffic(q, m):
            qs, ms = q - 1, m
            ql, ml = q + (m + 2) // RING, (m + 2) % RING
            for h in range(2):
                if not outside(qs, ms):
                    store(qs, ms, h)
                if not outside(ql, ml) and (not isinstance(ql, int) or ql > 0):
                    load(ql, ml, h)

        LOOP_SP = (N_PAIRS - 2 - RING) // RING
        for m in range(RING):
            traffic(0, m)
        with sp.Fori(1, 1 + LOOP_SP) as i:
            for m in range(RING):
                traffic(i, m)
        for b in range(RING * (1 + LOOP_SP), BODIES):
            traffic(b // RING, b % RING)

        after(pool, made["att"])
        owners = range(0, N_PAIRS, N_PAIRS // B)
        for m in range(RING):
            last = max(n for n in owners if n % RING == m)
            for h in range(2):
                pool.wait_ge(st[m][h], 16 * (last // RING + 1))
        acc = sem("acc")
        for b in range(B):
            for f in range(2):
                pool.dma_start(out[b, 0:LT, f * D // 2:(f + 1) * D // 2], att[f * RW + b * LT:f * RW + (b + 1) * LT, :],
                               accum_op=ALU.add).then_inc(acc, 16)
        pool.wait_ge(acc, 2 * 16 * B)
        for m in range(RING):
            for h in range(2):
                pool.wait_ge(st[m][h], 16 * len(range(m, N_PAIRS, RING)))


_INS = ['L0_attn_x', 'L0_attn_Wq', 'L0_attn_bq', 'L0_attn_Wk', 'L0_attn_Wv', 'L0_attn_bv', 'L0_attn_Wo', 'L0_attn_bo',
        'L0_attn_lna_w', 'L0_attn_lnc_w', 'L0_attn_lnd_w', 'L0_attn_Wlq', 'L0_attn_blq', 'L0_attn_Wlk', 'L0_attn_blk',
        'L0_attn_Wlv', 'L0_attn_blv', 'L0_attn_temp', 'L0_attn_threshold', 'L0_attn_factor',
        'L0_ffn_Win', 'L0_ffn_bin_', 'L0_ffn_W1', 'L0_ffn_b1', 'L0_ffn_W2', 'L0_ffn_b2', 'L0_ffn_Wout', 'L0_ffn_bout']


def kernel(**inputs):
    import numpy as _np
    import concourse.bacc as _bacc
    from concourse import mybir as _mybir
    from concourse.bass_utils import run_bass_kernel_spmd as _run

    nc = _bacc.Bacc("TRN2", target_bir_lowering=False, num_devices=1)
    arrays, args = {}, []
    for name in _INS:
        a = _np.ascontiguousarray(_np.atleast_1d(inputs[name]))
        arrays[f"in_{name}_dram"] = a
        args.append(nc.dram_tensor(f"in_{name}_dram", a.shape, _mybir.dt.from_np(a.dtype), kind="ExternalInput").ap())
    shape = inputs['L0_attn_x'].shape
    args.append(nc.dram_tensor("out_0_dram", shape, _mybir.dt.float32, kind="ExternalOutput").ap())
    residual_block(nc, *args)
    r = _run(nc, [arrays], core_ids=[0])
    return r.results[0]["out_0_dram"]
```
